# Optimizing a Trainium2 kernel written in Bass

```python
import numpy as np
import jax
import jax.numpy as jnp

def _softmax(x, axis=-1):
    return jax.nn.softmax(x, axis=axis)

def _gelu(x):
    return jax.nn.gelu(x, approximate=True)

def _silu(x):
    return jax.nn.silu(x)

def _sigmoid(x):
    return jax.nn.sigmoid(x)

def _layernorm(x, axis=-1, eps=1e-05):
    m = jnp.mean(x, axis=axis, keepdims=True)
    v = jnp.var(x, axis=axis, keepdims=True)
    return (x - m) / jnp.sqrt(v + eps)

def _scatter_add(tgt, idx, src, axis=0):
    return tgt.at[idx].add(src)

def _segment_sum(src, seg, n):
    return jax.ops.segment_sum(src, seg, n)
kernel_name = 'mk_xattn_ffn_d1_seqx_r4_0907f7'

def setup_inputs(seed: int=0):
    np.random.seed(seed)
    _w = jnp.asarray

    def _rec_inputs():
        import jax
        import jax.numpy as jnp
        _rk = jax.random.key(seed)
        x = 7.22e-05 + 1 * jax.random.normal(jax.random.fold_in(_rk, 1), (16, 112, 1024), jnp.float32)
        _lenS = 112 - jax.random.randint(jax.random.fold_in(_rk, 7), (16,), 0, max(1, 112 // 4) + 1, jnp.int32)
        _lenS2 = 375 - jax.random.randint(jax.random.fold_in(_rk, 8), (16,), 0, max(1, 375 // 4) + 1, jnp.int32)
        _ctx_4096P = jax.random.normal(jax.random.fold_in(_rk, 11), (16, 16, 1024), jnp.float32)
        _ctx_4096c = jax.random.dirichlet(jax.random.fold_in(_rk, 511), 0.3 * jnp.ones((16,), jnp.float32), (16, 375))
        _ctx_4096t = jnp.einsum('bsk,bkd->bsd', _ctx_4096c, _ctx_4096P)
        _ctx_4096t = _ctx_4096t * jax.lax.rsqrt(jnp.mean(jnp.square(_ctx_4096t)) + 1e-12) * 0.953939
        ctx_4096 = 4.13588e-05 + 0.999923 * (_ctx_4096t + 0.3 * jax.random.normal(jax.random.fold_in(_rk, 611), (16, 375, 1024), jnp.float32))
        return (x, ctx_4096)
    x, ctx_4096 = _rec_inputs()

    def _L0_xattn_setup():
        import jax, jax.numpy as jnp
        import numpy as np
        DIM = 1024
        NUM_HEADS = 32
        NUM_KV_HEADS = 8
        HEAD_DIM = DIM // NUM_HEADS
        KV_DIM = DIM // (NUM_HEADS // NUM_KV_HEADS)
        B, S = (1, 512)
        key = jax.random.key(seed)
        ks = jax.random.split(key, 7)
        w_scale = DIM ** (-0.5)
        return {'query': jax.random.normal(ks[0], (B, S, DIM), jnp.float32), 'key': jax.random.normal(ks[1], (B, S, DIM), jnp.float32), 'value': jax.random.normal(ks[2], (B, S, DIM), jnp.float32), 'Wq': jax.random.normal(ks[3], (DIM, DIM), jnp.float32) * w_scale, 'Wk': jax.random.normal(ks[4], (DIM, KV_DIM), jnp.float32) * w_scale, 'Wv': jax.random.normal(ks[5], (DIM, KV_DIM), jnp.float32) * w_scale, 'Wo': jax.random.normal(ks[6], (DIM, DIM), jnp.float32) * w_scale}
    _L0_xattn_all = _L0_xattn_setup()
    _L0_xattn_in = {k: v for k, v in _L0_xattn_all.items() if k in ('Wq', 'Wk', 'Wv', 'Wo')}
    del _L0_xattn_all

    def _L0_ffn_setup():
        import jax, jax.numpy as jnp
        import numpy as np
        BS = 128
        FP8_MAX = 448.0

        def act_quant(x):
            T, K = x.shape
            xb = x.reshape(T, K // BS, BS)
            amax = jnp.max(jnp.abs(xb), axis=-1)
            scale = amax / FP8_MAX + 1e-12
            xq = (xb / scale[:, :, None]).reshape(T, K)
            return (xq, scale)

        def linear_dsv3(x, wq, w_scale):
            T, K = x.shape
            N = wq.shape[0]
            xq, xs = act_quant(x)
            xdq = (xq.reshape(T, K // BS, BS) * xs[:, :, None]).reshape(T, K)
            wdq = (wq.reshape(N // BS, BS, K // BS, BS) * w_scale[:, None, :, None]).reshape(N, K)
            return xdq @ wdq.T
        key = jax.random.key(seed)
        ks = jax.random.split(key, 4)
        DIM, INTER = (1024, 3584)

        def make_qweight(k, n, m):
            w = jax.random.normal(k, (n, m), dtype=jnp.float32) * 0.02
            wb = w.reshape(n // BS, BS, m // BS, BS)
            amax = jnp.max(jnp.abs(wb), axis=(1, 3))
            scale = amax / FP8_MAX + 1e-12
            wq = (wb / scale[:, None, :, None]).reshape(n, m)
            return (wq, scale)
        x = jax.random.normal(ks[0], (2, 256, DIM), dtype=jnp.float32)
        w1, w1_scale = make_qweight(ks[1], INTER, DIM)
        w3, w3_scale = make_qweight(ks[2], INTER, DIM)
        w2, w2_scale = make_qweight(ks[3], DIM, INTER)
        return {'x': x, 'w1': w1, 'w1_scale': w1_scale, 'w3': w3, 'w3_scale': w3_scale, 'w2': w2, 'w2_scale': w2_scale}
    _L0_ffn_all = _L0_ffn_setup()
    _L0_ffn_in = {k: v for k, v in _L0_ffn_all.items() if k in ('w1', 'w1_scale', 'w3', 'w3_scale', 'w2', 'w2_scale')}
    del _L0_ffn_all
    return {'x': x, 'ctx_4096': ctx_4096, 'L0_xattn_Wq': _L0_xattn_in['Wq'], 'L0_xattn_Wk': _L0_xattn_in['Wk'], 'L0_xattn_Wv': _L0_xattn_in['Wv'], 'L0_xattn_Wo': _L0_xattn_in['Wo'], 'L0_ffn_w1': _L0_ffn_in['w1'], 'L0_ffn_w1_scale': _L0_ffn_in['w1_scale'], 'L0_ffn_w3': _L0_ffn_in['w3'], 'L0_ffn_w3_scale': _L0_ffn_in['w3_scale'], 'L0_ffn_w2': _L0_ffn_in['w2'], 'L0_ffn_w2_scale': _L0_ffn_in['w2_scale']}

def reference(x, ctx_4096, L0_xattn_Wq, L0_xattn_Wk, L0_xattn_Wv, L0_xattn_Wo, L0_ffn_w1, L0_ffn_w1_scale, L0_ffn_w3, L0_ffn_w3_scale, L0_ffn_w2, L0_ffn_w2_scale):
    import jax
    import jax.numpy as jnp

    def _L0_xattn_ref(query, key, value, Wq, Wk, Wv, Wo):
        import jax, jax.numpy as jnp
        import numpy as np
        DIM = 1024
        NUM_HEADS = 32
        NUM_KV_HEADS = 8
        HEAD_DIM = DIM // NUM_HEADS
        KV_DIM = DIM // (NUM_HEADS // NUM_KV_HEADS)
        B, S = (1, 512)
        b, sq, _ = query.shape
        _, sk, _ = key.shape
        rep = NUM_HEADS // NUM_KV_HEADS
        q = (query @ Wq).reshape(b, sq, NUM_HEADS, HEAD_DIM).transpose(0, 2, 1, 3)
        k = (key @ Wk).reshape(b, sk, NUM_KV_HEADS, HEAD_DIM).transpose(0, 2, 1, 3)
        v = (value @ Wv).reshape(b, sk, NUM_KV_HEADS, HEAD_DIM).transpose(0, 2, 1, 3)
        k = jnp.repeat(k, rep, axis=1)
        v = jnp.repeat(v, rep, axis=1)
        scale = HEAD_DIM ** (-0.5)
        scores = jnp.einsum('bhqd,bhkd->bhqk', q, k) * scale
        probs = jax.nn.softmax(scores, axis=-1)
        out = jnp.einsum('bhqk,bhkd->bhqd', probs, v)
        out = out.transpose(0, 2, 1, 3).reshape(b, sq, DIM)
        return out @ Wo

    def _L0_ffn_ref(x, w1, w1_scale, w3, w3_scale, w2, w2_scale):
        import jax, jax.numpy as jnp
        import numpy as np
        BS = 128
        FP8_MAX = 448.0

        def act_quant(x):
            T, K = x.shape
            xb = x.reshape(T, K // BS, BS)
            amax = jnp.max(jnp.abs(xb), axis=-1)
            scale = amax / FP8_MAX + 1e-12
            xq = (xb / scale[:, :, None]).reshape(T, K)
            return (xq, scale)

        def linear_dsv3(x, wq, w_scale):
            T, K = x.shape
            N = wq.shape[0]
            xq, xs = act_quant(x)
            xdq = (xq.reshape(T, K // BS, BS) * xs[:, :, None]).reshape(T, K)
            wdq = (wq.reshape(N // BS, BS, K // BS, BS) * w_scale[:, None, :, None]).reshape(N, K)
            return xdq @ wdq.T
        B, S, D = x.shape
        xf = x.reshape(-1, D)
        g = linear_dsv3(xf, w1, w1_scale)
        u = linear_dsv3(xf, w3, w3_scale)
        h = jax.nn.silu(g) * u
        y = linear_dsv3(h, w2, w2_scale)
        return y.reshape(B, S, D)
    x = x + _L0_xattn_ref(_layernorm(x, axis=-1), ctx_4096, ctx_4096, L0_xattn_Wq, L0_xattn_Wk, L0_xattn_Wv, L0_xattn_Wo)
    x = x + _L0_ffn_ref(_layernorm(x, axis=-1), L0_ffn_w1, L0_ffn_w1_scale, L0_ffn_w3, L0_ffn_w3_scale, L0_ffn_w2, L0_ffn_w2_scale)
    return x

_drawn_inputs = setup_inputs


def setup_inputs(seed=0):
    import zlib

    import numpy as np

    out = dict(_drawn_inputs(seed))
    spreads = {}
    factors = {'L0_ffn_w1_scale': 3.196, 'L0_ffn_w3_scale': 2.698, 'L0_ffn_w2_scale': 2.848}
    for name, (base, spread) in spreads.items():
        noise = np.random.default_rng([zlib.crc32(name.encode()), seed]).standard_normal(out[name].shape)
        drawn = base * np.exp(spread * noise) if base else spread * noise
        out[name] = jnp.asarray(drawn.astype(out[name].dtype))
    for name, factor in factors.items():
        out[name] = (out[name] * factor).astype(out[name].dtype)
    return out
```

```python
def build_program(nc, x, ctx, wq, wk, wv, wo, w1, w1_scale, w3, w3_scale, w2, w2_scale, out):
    import concourse.bass as bass
    from concourse import mybir
    from contextlib import ExitStack

    f32, f32r = mybir.dt.float32, mybir.dt.float32r
    ALU, AX, ACT = mybir.AluOpType, mybir.AxisListType, mybir.ActivationFunctionType

    P = 128
    B, SQ, D = x.shape
    SK = ctx.shape[1]
    KV = wk.shape[1]
    HD = 32
    NKV = KV // HD
    J = D // KV
    NH = NKV * J
    R = P // HD
    NG = NKV // R
    KT = D // P
    TOK = B * SQ
    GB = 4
    GT = GB * SQ
    CK = 125
    NC = SK // CK
    SKP = SK + 1
    INTER = w1.shape[0]
    NI = INTER // P
    HALF = TOK // 2
    TB = HALF // 2
    TT = HALF // P
    FB = 512
    EPS = 1e-5
    SCALE = HD ** -0.5
    assert NC * CK == SK and TT * P == HALF and GT <= FB and TB <= FB

    q_scr = nc.dram_tensor("q_scratch", [B, 2, P, NG, J * SQ], f32).ap()
    k_scr = nc.dram_tensor("k_scratch", [2, 2, NG, P, SKP], f32).ap()
    a_scr = nc.dram_tensor("attn_scratch", [P, NG * J, TOK], f32).ap()

    top = ExitStack()

    def sem(name):
        return top.enter_context(nc.semaphore(name))

    def split_product(pe, acc, lhs, rhs, first, last):
        (lh, ll), (rh, rl) = lhs, rhs
        pe.matmul(acc, lh, rh, start=first, stop=False)
        pe.matmul(acc, lh, rl, start=False, stop=False)
        return pe.matmul(acc, ll, rh, start=False, stop=last)

    def to_lo(dst, src, hi):
        return nc.vector.tensor_tensor(dst, src, hi.bitcast(f32), ALU.subtract)

    def wait(eng, s, value):
        if not isinstance(value, int) or value > 0:
            eng.wait_ge(s, value)

    with top:
        ident = top.enter_context(nc.sbuf_tensor("ident", [P, P], f32))
        neghalf = top.enter_context(nc.sbuf_tensor("neghalf", [P, 1], f32))
        bank = [top.enter_context(nc.psum_tensor(f"bank{i}", [P, FB], f32)) for i in range(8)]
        hold = top.enter_context(nc.sbuf_tensor("hold", [1, 3], f32))
        consts = sem("consts")

        def queries():
            with ExitStack() as st:
                def sb(name, shape, dt=f32):
                    return st.enter_context(nc.sbuf_tensor("q_" + name, shape, dt))
                wraw = sb("wraw", [P, KT, D])
                w_h, w_l = sb("w_h", [P, KT, NG * J, P], f32r), sb("w_l", [P, KT, NG * J, P], f32r)
                xin = sb("xin", [SQ, 2, D])
                stats, aggr = sb("stats", [SQ, 2, 6]), sb("aggr", [SQ, 2])
                veps, rstd = sb("veps", [SQ, 1]), sb("rstd", [SQ, 1])
                xn = sb("xn", [SQ, GB, D])
                xT_h, xT_l = sb("xT_h", [P, KT, GT], f32r), sb("xT_l", [P, KT, GT], f32r)
                q_h, q_l = sb("q_h", [P, NG * J, GT], f32r), sb("q_l", [P, NG * J, GT], f32r)
                w_loaded = [sem(f"q_w_loaded{g}") for g in range(NG)]
                w_hi, w_lo = sem("q_w_hi"), sem("q_w_lo")
                x_loaded = [sem("q_x_loaded0"), sem("q_x_loaded1")]
                stats_done, aggr_done, veps_done = sem("q_stats"), sem("q_aggr"), sem("q_veps")
                rstd_done, xn_done = sem("q_rstd"), sem("q_xn")
                t_done, xT_hi, xT_lo = sem("q_t_done"), sem("q_xT_hi"), sem("q_xT_lo")
                p_done, p_hi, p_lo = sem("q_p_done"), sem("q_p_hi"), sem("q_p_lo")
                q_stored = sem("q_stored")
                NGRP, C = B // GB, NG * J

                def perm(a, g):
                    return a[:, :, g * J * P:(g + 1) * J * P].rearrange(
                        "p k (r j d) -> p k j r d", r=R, j=J)

                def wcols(a, k, g):
                    return a[:, k, g * J:(g + 1) * J, :].rearrange("p j (r d) -> p j r d", r=R)

                with nc.Block() as block:
                    @block.sync
                    def _(sp):
                        wv_ = wq.rearrange("(k p) n -> p k n", p=P)

                        def load_x(t, slot):
                            sp.dma_start(xin[:, slot, :], x[bass.ds(t, 1)].rearrange(
                                "b q n -> q (b n)")).then_inc(x_loaded[slot], 16)
                        load_x(0, 0)
                        load_x(1, 1)
                        for g in range(NG):
                            cols = slice(g * J * P, (g + 1) * J * P)
                            sp.dma_start(wraw[:, :, cols], wv_[:, :, cols]).then_inc(w_loaded[g], 16)
                        with sp.Fori(0, B // 2 - 1) as i:
                            for par in range(2):
                                t = sp.snap(2 * i + par + 2)
                                sp.wait_ge(xn_done, 2 * i + par + 1)
                                load_x(t, par)

                    @block.gpsimd
                    def _(pool):
                        pool.memset(ident[:], 0.0).then_inc(consts, 1)
                        pool.memset(neghalf[:], -0.5).then_inc(consts, 1)
                        pool.wait_ge(consts, 2)
                        pool.affine_select(out=ident[:], in_=ident[:], compare_op=ALU.not_equal,
                                           fill=1.0, base=0, pattern=[[-1, P]],
                                           channel_multiplier=1).then_inc(consts, 1)
                        with pool.Fori(0, B) as t:
                            pool.wait_ge(veps_done, t + 1)
                            pool.tensor_tensor(rstd[:], veps[:], neghalf[0:SQ, :], ALU.pow
                                               ).then_inc(rstd_done, 1)

                    @block.vector
                    def _(dve):
                        def norm(t, slot, i):
                            dve.wait_ge(x_loaded[slot], 16 * (i + 1))
                            for h in range(2):
                                nc.vector.bn_stats(stats[:, h, :], xin[:, slot, h * FB:(h + 1) * FB]
                                                   ).then_inc(stats_done, 1)
                            dve.wait_ge(stats_done, 2 * t + 2)
                            nc.vector.memset(hold[:, 2:3], 0.0)
                            nc.vector.bn_aggr(aggr[:], stats[:]).then_inc(aggr_done, 1)
                            dve.wait_ge(aggr_done, t + 1)
                            nc.vector.tensor_scalar(veps[:], aggr[:, 1:2], EPS, None, ALU.add
                                                    ).then_inc(veps_done, 1)
                            dve.wait_ge(rstd_done, t + 1)

                        def norm_out(t, slot, dst):
                            nc.vector.tensor_scalar(xn[:, dst, :], xin[:, slot, :], aggr[:, 0:1],
                                                    rstd[:], ALU.subtract, ALU.mult
                                                    ).then_inc(xn_done, 1)

                        def norm_tile(grp, s):
                            t = GB * grp + s
                            norm(t, s % 2, 2 * grp + s // 2)
                            wait(dve, t_done, 2 * (t - GB) + 2)
                            norm_out(t, s % 2, s)

                        def group(grp, more):
                            for n in range(2 * GB):
                                s, kh = n // 2, n % 2
                                dve.wait_ge(xT_hi, 2 * GB * grp + n + 1)
                                to_lo(xT_l[:, 4 * kh:4 * kh + 4, s * SQ:(s + 1) * SQ],
                                      bank[n % 2][:, 0:4 * SQ].rearrange("p (k q) -> p k q", k=4),
                                      xT_h[:, 4 * kh:4 * kh + 4, s * SQ:(s + 1) * SQ]
                                      ).then_inc(xT_lo, 1)
                            for c in range(C):
                                dve.wait_ge(p_hi, C * grp + c + 1)
                                to_lo(q_l[:, c, :], bank[2 + c % 2][:, 0:GT], q_h[:, c, :]
                                      ).then_inc(p_lo, 1)
                                if more and c % 2:
                                    norm_tile(grp + 1, c // 2)

                        for s in range(GB):
                            norm_tile(0, s)
                        for g in range(NG):
                            for k in range(KT):
                                dve.wait_ge(w_hi, KT * g + k + 1)
                                to_lo(wcols(w_l, k, g), perm(wraw, g)[:, k], wcols(w_h, k, g)
                                      ).then_inc(w_lo, 1)
                        with dve.Fori(0, NGRP - 1) as grp:
                            group(grp, True)
                        group(NGRP - 1, False)

                    @block.scalar
                    def _(act):
                        for g in range(NG):
                            act.wait_ge(w_loaded[g], 16)
                            for k in range(KT):
                                nc.scalar.activation(wcols(w_h, k, g), perm(wraw, g)[:, k], ACT.Copy
                                                     ).then_inc(w_hi, 1)

                        def group(grp):
                            for n in range(2 * GB):
                                s, kh = n // 2, n % 2
                                act.wait_ge(t_done, 2 * GB * grp + n + 1)
                                if n == 0:
                                    wait(act, p_done, C * grp)
                                nc.scalar.activation(
                                    xT_h[:, 4 * kh:4 * kh + 4, s * SQ:(s + 1) * SQ],
                                    bank[n % 2][:, 0:4 * SQ].rearrange("p (k q) -> p k q", k=4),
                                    ACT.Copy).then_inc(xT_hi, 1)
                            wait(act, q_stored, 16 * 2 * GB * grp)
                            for c in range(C):
                                act.wait_ge(p_done, C * grp + c + 1)
                                nc.scalar.activation(q_h[:, c, :], bank[2 + c % 2][:, 0:GT],
                                                     ACT.Copy).then_inc(p_hi, 1)
                            act.wait_ge(p_lo, C * grp + C)
                            for s in range(GB):
                                for hl, buf in enumerate((q_h, q_l)):
                                    act.dma_start(
                                        q_scr[bass.ds(GB * grp + s, 1), hl].rearrange(
                                            "b p g (j q) -> p (b g j) q", j=J),
                                        buf[:, :, s * SQ:(s + 1) * SQ].bitcast(f32)
                                        ).then_inc(q_stored, 16)
                        group(0)
                        with act.Fori(1, NGRP) as grp:
                            group(grp)
                        act.wait_ge(q_stored, 16 * 2 * B)

                    @block.tensor
                    def _(pe):
                        pe.wait_ge(consts, 3)
                        with pe.Fori(0, NGRP) as grp:
                            for n in range(2 * GB):
                                s, kh = n // 2, n % 2
                                pe.wait_ge(xn_done, GB * grp + s + 1)
                                if n >= 2:
                                    pe.wait_ge(xT_lo, 2 * GB * grp + n - 1)
                                for k in range(4):
                                    last = pe.transpose(
                                        bank[n % 2][:, k * SQ:(k + 1) * SQ],
                                        xn[:, s, (4 * kh + k) * P:(4 * kh + k + 1) * P],
                                        ident[0:SQ, 0:SQ])
                                last.then_inc(t_done, 1)
                            pe.wait_ge(xT_lo, 2 * GB * grp + 2 * GB)
                            for c in range(C):
                                if c % J == 0:
                                    pe.wait_ge(w_lo, KT * (c // J + 1))
                                if c >= 2:
                                    pe.wait_ge(p_lo, C * grp + c - 1)
                                for k in range(KT):
                                    last = split_product(
                                        pe, bank[2 + c % 2][:, 0:GT],
                                        (w_h[:, k, c, :], w_l[:, k, c, :]),
                                        (xT_h[:, k, :], xT_l[:, k, :]), k == 0, k == KT - 1)
                                last.then_inc(p_done, 1)

        def attention():
            with ExitStack() as st:
                def sb(name, shape, dt=f32):
                    return st.enter_context(nc.sbuf_tensor("a_" + name, shape, dt))
                w_h, w_l = sb("w_h", [P, KT, 2 * KV], f32r), sb("w_l", [P, KT, 2 * KV], f32r)
                cin = sb("cin", [CK, 2, NC, D])
                cT_h, cT_l = sb("cT_h", [P, KT, SKP], f32r), sb("cT_l", [P, KT, SKP], f32r)
                k_h, k_l = sb("k_h", [P, NG, SKP], f32r), sb("k_l", [P, NG, SKP], f32r)
                kst = sb("kst", [98, 2, NKV, SKP], f32r)
                qst = sb("qst", [98, 2, NKV, J * SQ], f32r)
                vnew, v = sb("vnew", [CK, NC, KV]), sb("v", [CK, 2, NC, KV])
                pr = sb("pr", [P, NG, R, NC, J * SQ])
                o, l = sb("o", [P, NG, J * SQ]), sb("l", [P, NG, J * SQ])
                nm = sb("nm", [SQ, 2, NH])
                nm_h, nm_l = sb("nm_h", [NH, SQ], f32r), sb("nm_l", [NH, SQ], f32r)
                ones = sb("ones", [CK, HD])
                wraw = pr[:, :, :, :, :].rearrange("p g r c n -> p (g r c n)")[
                    :, 0:KT * 2 * KV].rearrange("p (k n) -> p k n", k=KT)

                s_bank, st_bank, pj_bank = bank[0:2], bank[2:4], bank[4:6]
                o_bank, l_bank = bank[6], bank[7]
                w_loaded, w_hi, w_lo = sem("a_w_loaded"), sem("a_w_hi"), sem("a_w_lo")
                ready = sem("a_consts")
                c_loaded = [sem("a_c_loaded0"), sem("a_c_loaded1")]
                t_done, t_hi, t_lo = sem("a_t_done"), sem("a_t_hi"), sem("a_t_lo")
                k_done, k_hi, k_lo = sem("a_k_done"), sem("a_k_hi"), sem("a_k_lo")
                v_done, v_out, v_moved = sem("a_v_done"), sem("a_v_out"), sem("a_v_moved")
                k_stored = sem("a_k_stored")
                kq_loaded = [[sem(f"a_kq_loaded{s}{g}") for g in range(NG)] for s in range(2)]
                s_done, max_done = sem("a_s_done"), sem("a_max_done")
                nmT_done, nm_hi, nm_lo = sem("a_nmT_done"), sem("a_nm_hi"), sem("a_nm_lo")
                nm_loaded = [sem("a_nm_loaded0"), sem("a_nm_loaded1")]
                st_done, exp_done, pv_done = sem("a_st_done"), sem("a_exp_done"), sem("a_pv_done")
                o_copied, l_inverted, o_scaled = sem("a_o_copied"), sem("a_l_inv"), sem("a_o_scaled")
                o_stored = [sem(f"a_o_stored{g}") for g in range(NG)]

                NT = 2 * NC
                NU = NG * NC * R

                STEPS, K0, V0, U0 = 32, 7, 15, 5
                HEADS, h0 = [], 0
                for s in range(STEPS):
                    n = (s + 1) % 2 if s < U0 else 2 if s in (8, 11) else 1
                    HEADS.append(range(h0, h0 + n))
                    h0 += n
                assert h0 == NH
                PV = {}
                for g in range(NG):
                    for c in range(NC):
                        at = U0 + R * (NC * g + c + 1) + 1
                        PV[at], PV[at + 1] = (g, c, False), (g, c, True)
                INV = {21: (0, 0), 23: (0, 1), 25: (0, 2), 27: (0, 3),
                       6: (1, 0), 8: (1, 1), 10: (1, 2), 12: (1, 3)}
                def each(eng, body):
                    body(-1, 0, True, False, False)
                    body(-1, 1, True, True, False)
                    body(0, 0, True, True, True)
                    body(0, 1, True, True, True)
                    with eng.Fori(1, B // 2 - 1) as i:
                        body(i, 0, True, True, True)
                        body(i, 1, True, True, True)
                    body(B // 2 - 1, 0, False, True, True)
                    body(B // 2 - 1, 1, False, False, True)

                with nc.Block() as block:
                    @block.sync
                    def _(sp):
                        def load_ctx(n, slot):
                            for c in range(NC):
                                sp.dma_start(cin[:, slot, c, :], ctx[bass.ds(n, 1), c * CK:(c + 1) * CK, :]
                                             .rearrange("b k n -> k (b n)")
                                             ).then_inc(c_loaded[slot], 16)
                        load_ctx(0, 0)
                        sp.dma_start(wraw[:, :, 0:KV], wk.rearrange("(k p) n -> p k n", p=P)
                                     ).then_inc(w_loaded, 16)
                        sp.dma_start(wraw[:, :, KV:2 * KV], wv.rearrange("(k p) n -> p k n", p=P)
                                     ).then_inc(w_loaded, 16)
                        load_ctx(1, 1)

                        def body(i, par, proj, score, attn):
                            b = 2 * i + par
                            pb = b + 2
                            if attn:
                                sp.wait_ge(nm_lo, b + 1)
                                for row, src in ((96, nm_h), (97, nm_l)):
                                    sp.dma_start(qst[row:row + 1, par, :, :].bitcast(f32).rearrange(
                                        "o g (j q) -> o (g j) q", j=J), src[:, :].bitcast(f32)
                                        ).then_inc(nm_loaded[par], 16)
                            if proj and not (isinstance(b, int) and b == -2):
                                load_next = not (isinstance(b, int)) or b + 3 < B
                                if load_next:
                                    sp.wait_ge(t_done, NT * (b + 2))
                                    load_ctx_clamped(b, par)
                            if proj:
                                sp.wait_ge(k_lo, NG * (pb + 1))
                                for hl, buf in enumerate((k_h, k_l)):
                                    sp.dma_start(k_scr[par, hl].rearrange("g p n -> p g n"),
                                                 buf[:, :, :].bitcast(f32)).then_inc(k_stored, 16)
                                sp.wait_ge(k_stored, 32 * (pb + 1))
                                for g in range(NG):
                                    wait(sp, st_done, NU * b + NC * R * (g + 1))
                                    heads = slice(g * R, (g + 1) * R)
                                    for m, (khl, qhl) in enumerate(((0, 0), (1, 0), (0, 1))):
                                        rows = slice(m * HD, (m + 1) * HD)
                                        sp.dma_start(kst[rows, par, heads, :].bitcast(f32),
                                                     k_scr[par, khl, g].rearrange(
                                                         "(r d) n -> d r n", r=R)
                                                     ).then_inc(kq_loaded[par][g], 16)
                                        sp.dma_start(qst[rows, par, heads, :].bitcast(f32),
                                                     q_scr[bass.ds(pb, 1), qhl, :, g].rearrange(
                                                         "b (r d) n -> d (b r) n", r=R)
                                                     ).then_inc(kq_loaded[par][g], 16)

                        def load_ctx_clamped(b, par):
                            load_ctx(b + 3, 1 - par)

                        body(-1, 0, True, False, False)
                        body(-1, 1, True, True, False)
                        body(0, 0, True, True, True)
                        body(0, 1, True, True, True)
                        with sp.Fori(1, B // 2 - 2) as i:
                            body(i, 0, True, True, True)
                            body(i, 1, True, True, True)
                        body(B // 2 - 2, 0, True, True, True)
                        body(B // 2 - 2, 1, True, True, True)
                        body(B // 2 - 1, 0, False, True, True)
                        body(B // 2 - 1, 1, False, False, True)

                    @block.gpsimd
                    def _(pool):
                        pool.memset(ones[:], 1.0).then_inc(ready, 1)
                        pool.wait_ge(ready, 1)
                        pool.memset(kst[96:98, :, :, :].bitcast(f32).rearrange("p s g n -> p (s g n)"), 1.0
                                    ).then_inc(ready, 1)
                        pool.wait_ge(ready, 2)
                        pool.memset(cT_h[:, :, SK:SKP].bitcast(f32), 0.0).then_inc(ready, 1)
                        pool.memset(cT_l[:, :, SK:SKP].bitcast(f32), 0.0).then_inc(ready, 1)

                        def body(i, par, proj, score, attn):
                            b = 2 * i + par
                            if attn:
                                for g in range(NG):
                                    pool.wait_ge(l_inverted, J * (NG * b + g + 1))
                                    pool.tensor_tensor(o[:, g, :], o[:, g, :], l[:, g, :],
                                                       ALU.mult).then_inc(o_scaled, 1)
                                    pool.wait_ge(o_scaled, NG * b + g + 1)
                                    pool.dma_start(
                                        a_scr[:, g * J:(g + 1) * J, bass.ds(b * SQ, SQ)],
                                        o[:, g, :].rearrange("p (j q) -> p j q", j=J)
                                    ).then_inc(o_stored[g], 16)
                        each(pool, body)
                        for g in range(NG):
                            pool.wait_ge(o_stored[g], 16 * B)

                    @block.vector
                    def _(dve):
                        for k in range(KT):
                            dve.wait_ge(w_hi, k + 1)
                            to_lo(w_l[:, k, :], wraw[:, k, :], w_h[:, k, :]).then_inc(w_lo, 1)

                        def invert(b, g, j):
                            dve.wait_ge(o_copied, 2 * (NG * b + g + 1))
                            part = l[:, g, j * SQ:(j + 1) * SQ]
                            nc.vector.reciprocal(part, part).then_inc(l_inverted, 1)

                        def body(i, par, proj, score, attn):
                            b = 2 * i + par
                            sb_, pb = b + 1, b + 2
                            for s in range(STEPS):
                                if proj and s < NT:
                                    c, kh = s // 2, s % 2
                                    dve.wait_ge(t_hi, NT * pb + s + 1)
                                    dst = (slice(None), slice(4 * kh, 4 * kh + 4),
                                           slice(c * CK, (c + 1) * CK))
                                    n = s if s == 0 else s + 1
                                    to_lo(cT_l[dst], pj_bank[n % 2][:, 0:4 * CK].rearrange(
                                        "p (k n) -> p k n", k=4), cT_h[dst]).then_inc(t_lo, 1)
                                if attn and s == 0:
                                    dve.wait_ge(nmT_done, b + 1)
                                    wait(dve, nm_loaded[1 - par], 32 * (i + par))
                                    nc.vector.tensor_copy(nm_h[:], pj_bank[1][0:NH, 0:SQ]
                                                          ).then_inc(nm_hi, 1)
                                    dve.wait_ge(nm_hi, b + 1)
                                    to_lo(nm_l[:], pj_bank[1][0:NH, 0:SQ], nm_h[:]
                                          ).then_inc(nm_lo, 1)
                                if score:
                                    for h in HEADS[s]:
                                        dve.wait_ge(s_done, NH * sb_ + h + 1)
                                        nc.vector.tensor_reduce(nm[:, 1 - par, h:h + 1],
                                                                s_bank[h % 2][0:SQ, 0:SK], AX.X,
                                                                ALU.max, negate=True
                                                                ).then_inc(max_done, 1)
                                if score and s == 9:
                                    dve.wait_ge(v_out, NC * (sb_ + 1))
                                    wait(dve, pv_done, NG * b)
                                    nc.vector.tensor_copy(v[:, 1 - par, :, :], vnew[:, :, :]
                                                          ).then_inc(v_moved, 1)
                                if proj and s in (K0 + 3, K0 + 7):
                                    g = (s - K0) // 4
                                    dve.wait_ge(k_hi, NG * pb + g + 1)
                                    to_lo(k_l[:, g, :], pj_bank[(7 + g) % 2][:, 0:SKP],
                                          k_h[:, g, :]).then_inc(k_lo, 1)
                                if proj and s in (V0 + 3, V0 + 7, V0 + 11):
                                    c = (s - V0) // 4
                                    dve.wait_ge(v_done, NC * pb + c + 1)
                                    if c == 0:
                                        wait(dve, v_moved, pb)
                                    nc.vector.tensor_copy(vnew[:, c, :],
                                                          pj_bank[(9 + c) % 2][0:CK, 0:KV]
                                                          ).then_inc(v_out, 1)
                                if attn and s in INV:
                                    g, j = INV[s]
                                    if g == 0:
                                        invert(b, 0, j)
                                    elif not (isinstance(b, int) and b == 0):
                                        invert(b - 1, 1, j)
                        each(dve, body)
                        for j in range(J):
                            invert(B - 1, 1, j)

                    @block.scalar
                    def _(act):
                        act.wait_ge(w_loaded, 32)
                        for k in range(KT):
                            nc.scalar.activation(w_h[:, k, :], wraw[:, k, :], ACT.Copy
                                                 ).then_inc(w_hi, 1)

                        def copy_out(b, g):
                            act.wait_ge(pv_done, NG * b + g + 1)
                            wait(act, o_stored[g], 16 * b)
                            nc.scalar.activation(o[:, g, :], o_bank[:, 0:J * SQ], ACT.Copy
                                                 ).then_inc(o_copied, 1)
                            nc.scalar.activation(l[:, g, :], l_bank[:, 0:J * SQ], ACT.Copy
                                                 ).then_inc(o_copied, 1)

                        def body(i, par, proj, score, attn):
                            b = 2 * i + par
                            pb = b + 2
                            for s in range(STEPS):
                                if proj and s < NT:
                                    c, kh = s // 2, s % 2
                                    act.wait_ge(t_done, NT * pb + s + 1)
                                    if s == 0:
                                        wait(act, v_done, NC * pb)
                                    n = s if s == 0 else s + 1
                                    nc.scalar.activation(
                                        cT_h[:, 4 * kh:4 * kh + 4, c * CK:(c + 1) * CK],
                                        pj_bank[n % 2][:, 0:4 * CK].rearrange(
                                            "p (k n) -> p k n", k=4), ACT.Copy).then_inc(t_hi, 1)
                                if attn and s == 4 and not (isinstance(b, int) and b == 0):
                                    copy_out(b - 1, 1)
                                if proj and s in (K0 + 3, K0 + 7):
                                    g = (s - K0) // 4
                                    act.wait_ge(k_done, NG * pb + g + 1)
                                    if g == 0:
                                        wait(act, k_stored, 32 * pb)
                                    nc.scalar.activation(k_h[:, g, :],
                                                         pj_bank[(7 + g) % 2][:, 0:SKP], ACT.Copy
                                                         ).then_inc(k_hi, 1)
                                if attn and 0 <= s - U0 < NU:
                                    u = s - U0
                                    g, c, r = u // (NC * R), u // R % NC, u % R
                                    act.wait_ge(st_done, NU * b + u + 1)
                                    if c == 0 and r == 0:
                                        wait(act, pv_done, NG * (b - 1) + g + 1)
                                    nc.scalar.activation(pr[0:CK, g, r, c, :],
                                                         st_bank[u % 2][0:CK, 0:J * SQ], ACT.Exp,
                                                         scale=SCALE).then_inc(exp_done, 1)
                                if attn and s == 20:
                                    copy_out(b, 0)
                        each(act, body)
                        copy_out(B - 1, 1)

                    @block.tensor
                    def _(pe):
                        pe.wait_ge(ready, 4)

                        def body(i, par, proj, score, attn):
                            b = 2 * i + par
                            sb_, pb = b + 1, b + 2
                            for s in range(STEPS):
                                for h in HEADS[s] if score else ():
                                    g, j = h // J, h % J
                                    if h % (NH // NG) == 0:
                                        pe.wait_ge(kq_loaded[1 - par][h * NG // NH],
                                                   96 * (i + par + 1))
                                    wait(pe, max_done, NH * sb_ + h - 1)
                                    pe.matmul(s_bank[h % 2][0:SQ, 0:SKP],
                                              qst[0:96, 1 - par, g, j * SQ:(j + 1) * SQ],
                                              kst[0:96, 1 - par, g, :], start=True, stop=True
                                              ).then_inc(s_done, 1)
                                if proj and s < NT:
                                    c, kh = s // 2, s % 2
                                    if s == 0:
                                        pe.wait_ge(c_loaded[par], 16 * NC * (i + 2))
                                        wait(pe, v_out, NC * pb - 1)
                                    elif s == 2 and attn:
                                        pe.wait_ge(nm_lo, b + 1)
                                    elif s == 2:
                                        wait(pe, v_out, NC * pb)
                                    else:
                                        pe.wait_ge(t_lo, NT * pb + (1 if s == 1 else s - 1))
                                    n = s if s == 0 else s + 1
                                    for k in range(4):
                                        kk = 4 * kh + k
                                        last = pe.transpose(pj_bank[n % 2][:, k * CK:(k + 1) * CK],
                                                            cin[:, par, c, kk * P:(kk + 1) * P],
                                                            ident[0:CK, 0:CK])
                                    last.then_inc(t_done, 1)
                                if attn and s == 0:
                                    pe.wait_ge(max_done, NH * (b + 1))
                                    done = NC * (b + 2)
                                    pe.wait_ge(v_out, min(done, NC * B) if isinstance(done, int)
                                               else done)
                                    pe.transpose(pj_bank[1][0:NH, 0:SQ], nm[:, par, :],
                                                 ident[0:SQ, 0:SQ]).then_inc(nmT_done, 1)
                                if proj and K0 <= s < K0 + 8:
                                    g, k0 = (s - K0) // 4, 2 * ((s - K0) % 4)
                                    if s == K0:
                                        wait(pe, w_lo, KT)
                                        pe.wait_ge(t_lo, NT * (pb + 1))
                                    for k in range(k0, k0 + 2):
                                        last = split_product(
                                            pe, pj_bank[(7 + g) % 2][:, 0:SKP],
                                            (w_h[:, k, g * P:(g + 1) * P], w_l[:, k, g * P:(g + 1) * P]),
                                            (cT_h[:, k, :], cT_l[:, k, :]), k == 0, k == KT - 1)
                                    if k0 == KT - 2:
                                        last.then_inc(k_done, 1)
                                if proj and V0 <= s < V0 + 12:
                                    c, k0 = (s - V0) // 4, 2 * ((s - V0) % 4)
                                    keys = slice(c * CK, (c + 1) * CK)
                                    if k0 == 0:
                                        if c < 2:
                                            pe.wait_ge(k_lo, NG * pb + c + 1)
                                        else:
                                            pe.wait_ge(v_out, NC * pb + 1)
                                    for k in range(k0, k0 + 2):
                                        last = split_product(
                                            pe, pj_bank[(9 + c) % 2][0:CK, 0:KV],
                                            (cT_h[:, k, keys], cT_l[:, k, keys]),
                                            (w_h[:, k, KV:2 * KV], w_l[:, k, KV:2 * KV]),
                                            k == 0, k == KT - 1)
                                    if k0 == KT - 2:
                                        last.then_inc(v_done, 1)
                                if attn and 0 <= s - U0 < NU:
                                    u = s - U0
                                    g, c, r = u // (NC * R), u // R % NC, u % R
                                    if u == 0:
                                        pe.wait_ge(nm_loaded[par], 32 * (i + 1))
                                    wait(pe, exp_done, NU * b + u - 1)
                                    pe.matmul(st_bank[u % 2][0:CK, 0:J * SQ],
                                              kst[0:98, par, g * R + r, c * CK:(c + 1) * CK],
                                              qst[0:98, par, g * R + r, :], start=True, stop=True
                                              ).then_inc(st_done, 1)
                                if attn and s in PV:
                                    g, c, one = PV[s]
                                    if c == 0 and not one:
                                        wait(pe, o_copied, 2 * (NG * b + g))
                                        pe.wait_ge(v_moved, b + 1)
                                    pe.wait_ge(exp_done, NU * b + R * (NC * g + c + 1))
                                    for r in range(R):
                                        h = (g * R + r) * HD
                                        last = pe.matmul(
                                            (l_bank if one else o_bank)[r * HD:(r + 1) * HD,
                                                                        0:J * SQ],
                                            ones[:, :] if one else v[:, par, c, h:h + HD],
                                            pr[0:CK, g, r, c, :], start=c == 0, stop=c == NC - 1)
                                    if one and c == NC - 1:
                                        last.then_inc(pv_done, 1)
                        each(pe, body)

        def mixing(half, y, x2_h, x2_l):
            with ExitStack() as st:
                C = NG * J

                def sb(name, shape, dt=f32):
                    return st.enter_context(nc.sbuf_tensor(f"m{half}_{name}", shape, dt))

                def s_(name):
                    return sem(f"m{half}_{name}")
                wraw = sb("wraw", [P, 2, D])
                w_h, w_l = sb("w_h", [P, C, D], f32r), sb("w_l", [P, C, D], f32r)
                ain = sb("ain", [P, 2, C, P])
                a_h, a_l = sb("a_h", [P, 2, C, P], f32r), sb("a_l", [P, 2, C, P], f32r)
                xin, xn = sb("xin", [P, 2, D]), sb("xn", [P, 2, D])
                stats, aggr = sb("stats", [P, 2, 6]), sb("aggr", [P, 2])
                veps, rstd = sb("veps", [P, 1]), sb("rstd", [P, 1])
                w_loaded = [s_("w_loaded0"), s_("w_loaded1")]
                w_hi, w_lo = s_("w_hi"), s_("w_lo")
                a_loaded = [s_("a_loaded0"), s_("a_loaded1")]
                x_loaded = [s_("x_loaded0"), s_("x_loaded1")]
                a_hi, a_lo = s_("a_hi"), s_("a_lo")
                o_done, y_done = s_("o_done"), s_("y_done")
                stats_done, aggr_done, veps_done = s_("stats"), s_("aggr"), s_("veps")
                rstd_done, xn_done = s_("rstd"), s_("xn")
                t_done, t_hi, t_lo = s_("t_done"), s_("t_hi"), s_("t_lo")
                o_bank, t_bank = bank[0:2], bank[2:4]
                xf = x.rearrange("b q n -> (b q) n")
                wo_v = wo.rearrange("(g r j d) n -> g j r d n", g=NG, r=R, j=J)

                def tiles(eng, step):
                    step(1, 1, 0)
                    with eng.Fori(1, TT // 2) as i:
                        step(2 * i, 0, i)
                        step(2 * i + 1, 1, i)
                    step(TT - 1, 0, TT // 2)

                with nc.Block() as block:
                    @block.sync
                    def _(sp):
                        def load(t, slot):
                            tok = half * HALF + t * P
                            sp.dma_start(ain[:, slot, :, :], a_scr[:, :, bass.ds(tok, P)]
                                         ).then_inc(a_loaded[slot], 16)
                            sp.dma_start(xin[:, slot, :], xf[bass.ds(tok, P), :]
                                         ).then_inc(x_loaded[slot], 16)
                        load(0, 0)
                        for c in range(C):
                            if c >= 2:
                                sp.wait_ge(w_lo, c - 1)
                            for r in range(R):
                                sp.dma_start(wraw[r * HD:(r + 1) * HD, c % 2, :],
                                             wo_v[c // J, c % J, r]).then_inc(w_loaded[c % 2], 16)
                        load(1, 1)
                        with sp.Fori(0, TT // 2 - 1) as i:
                            for t, slot in ((2 * i + 2, 0), (2 * i + 3, 1)):
                                sp.wait_ge(y_done, 2 * (t - 1))
                                load(t, slot)
                        sp.wait_ge(y_done, 2 * (TT - 2))
                        load(TT - 1, 0)

                    @block.gpsimd
                    def _(pool):
                        with pool.Fori(0, TT) as t:
                            pool.wait_ge(veps_done, t + 1)
                            pool.tensor_tensor(rstd[:], veps[:], neghalf[:], ALU.pow
                                               ).then_inc(rstd_done, 1)

                    @block.scalar
                    def _(act):
                        def split_attention(t, slot, use):
                            act.wait_ge(a_loaded[slot], 16 * (use + 1))
                            wait(act, o_done, 2 * (t - 1))
                            nc.scalar.activation(a_h[:, slot, :, :], ain[:, slot, :, :], ACT.Copy
                                                 ).then_inc(a_hi, 1)

                        def split_x(t):
                            for kh in range(2):
                                act.wait_ge(t_done, 2 * t + kh + 1)
                                nc.scalar.activation(
                                    x2_h[:, 4 * kh:4 * kh + 4, bass.ds(t * P, P)],
                                    t_bank[kh][:, :].rearrange("p (k q) -> p k q", k=4), ACT.Copy
                                ).then_inc(t_hi, 1)
                        split_attention(0, 0, 0)
                        for c in range(C):
                            act.wait_ge(w_loaded[c % 2], 16 * R * (c // 2 + 1))
                            nc.scalar.activation(w_h[:, c, :], wraw[:, c % 2, :], ACT.Copy
                                                 ).then_inc(w_hi, 1)
                        split_attention(1, 1, 0)

                        def step(t, slot, use):
                            if not (isinstance(t, int) and t == TT - 1):
                                split_attention(t + 1, 1 - slot, use + slot)
                            split_x(t - 1)
                        tiles(act, step)
                        split_x(TT - 1)

                    @block.vector
                    def _(dve):
                        def split_attention(t, slot):
                            dve.wait_ge(a_hi, t + 1)
                            to_lo(a_l[:, slot, :, :], ain[:, slot, :, :], a_h[:, slot, :, :]
                                  ).then_inc(a_lo, 1)

                        def residual_norm(t, slot, use):
                            dve.wait_ge(x_loaded[slot], 16 * (use + 1))
                            for n in range(2):
                                cols = slice(n * FB, (n + 1) * FB)
                                dve.wait_ge(o_done, 2 * t + n + 1)
                                nc.vector.tensor_tensor(y[:, bass.ds(t, 1), cols].rearrange(
                                    "p t n -> p (t n)"), o_bank[n][:, :],
                                    xin[:, slot, cols], ALU.add).then_inc(y_done, 1)
                            for n in range(2):
                                cols = slice(n * FB, (n + 1) * FB)
                                dve.wait_ge(y_done, 2 * t + n + 1)
                                nc.vector.memset(hold[:, n:n + 1], 0.0)
                                nc.vector.bn_stats(stats[:, n, :], y[:, bass.ds(t, 1), cols].rearrange(
                                    "p t n -> p (t n)")).then_inc(stats_done, 1)
                            dve.wait_ge(stats_done, 2 * t + 2)
                            nc.vector.memset(hold[:, 2:3], 0.0)
                            nc.vector.bn_aggr(aggr[:], stats[:]).then_inc(aggr_done, 1)
                            dve.wait_ge(aggr_done, t + 1)
                            nc.vector.tensor_scalar(veps[:], aggr[:, 1:2], EPS, None, ALU.add
                                                    ).then_inc(veps_done, 1)
                            dve.wait_ge(rstd_done, t + 1)
                            wait(dve, t_done, 2 * (t - 1))
                            nc.vector.tensor_scalar(xn[:, slot, :], y[:, bass.ds(t, 1), :].rearrange(
                                "p t n -> p (t n)"), aggr[:, 0:1], rstd[:], ALU.subtract, ALU.mult
                                ).then_inc(xn_done, 1)

                        def split_x(t):
                            for kh in range(2):
                                dst = (slice(None), slice(4 * kh, 4 * kh + 4), bass.ds(t * P, P))
                                dve.wait_ge(t_hi, 2 * t + kh + 1)
                                to_lo(x2_l[dst], t_bank[kh][:, :].rearrange(
                                    "p (k q) -> p k q", k=4), x2_h[dst]).then_inc(t_lo, 1)
                        split_attention(0, 0)
                        for c in range(C):
                            dve.wait_ge(w_hi, c + 1)
                            to_lo(w_l[:, c, :], wraw[:, c % 2, :], w_h[:, c, :]).then_inc(w_lo, 1)
                        split_attention(1, 1)
                        residual_norm(0, 0, 0)

                        def step(t, slot, use):
                            if not (isinstance(t, int) and t == TT - 1):
                                split_attention(t + 1, 1 - slot)
                            residual_norm(t, slot, use)
                            split_x(t - 1)
                        tiles(dve, step)
                        split_x(TT - 1)

                    @block.tensor
                    def _(pe):
                        def products(t, slot, first):
                            pe.wait_ge(a_lo, t + 1)
                            for n in range(2):
                                wait(pe, y_done, 2 * t + n - 1)
                                for c in range(C):
                                    if first and n == 0:
                                        pe.wait_ge(w_lo, c + 1)
                                    cols = slice(n * FB, (n + 1) * FB)
                                    last = split_product(
                                        pe, o_bank[n][:, :],
                                        (a_h[:, slot, c, :], a_l[:, slot, c, :]),
                                        (w_h[:, c, cols], w_l[:, c, cols]), c == 0, c == C - 1)
                                last.then_inc(o_done, 1)

                        def transposes(t, slot):
                            pe.wait_ge(xn_done, t + 1)
                            for kh in range(2):
                                wait(pe, t_lo, 2 * t + kh - 1)
                                for k in range(4):
                                    kk = 4 * kh + k
                                    last = pe.transpose(t_bank[kh][:, k * P:(k + 1) * P],
                                                        xn[:, slot, kk * P:(kk + 1) * P], ident[:])
                                last.then_inc(t_done, 1)
                        products(0, 0, True)

                        def step(t, slot, use):
                            products(t, slot, False)
                            transposes(t - 1, 1 - slot)
                        tiles(pe, step)
                        transposes(TT - 1, 0)

        def ffn(half, y, x2_h, x2_l):
            with ExitStack() as st:
                def sb(name, shape, dt=f32):
                    return st.enter_context(nc.sbuf_tensor(f"f{half}_{name}", shape, dt))

                def s_(name):
                    return sem(f"f{half}_{name}")
                raw13, raw2 = sb("raw13", [P, 2, 2, D]), sb("raw2", [P, 2, KT, P])
                sc13, sc2 = sb("sc13", [P, 2, NI, KT]), sb("sc2", [P, KT, NI])
                w13_h = sb("w13_h", [P, 2, 2, KT, P], f32r)
                w13_l = sb("w13_l", [P, 2, 2, KT, P], f32r)
                w2_h, w2_l = sb("w2_h", [P, 2, D], f32r), sb("w2_l", [P, 2, D], f32r)
                gate, hf = sb("gate", [P, 2, TB]), sb("hf", [P, 2, TB])
                h_h, h_l = sb("h_h", [P, 2, HALF], f32r), sb("h_l", [P, 2, HALF], f32r)
                g_bank, u_bank, y_bank, t_bank = bank[0:2], bank[2:4], bank[4:6], bank[6:8]
                sc_loaded = s_("sc_loaded")
                r13_loaded = [s_("r13_loaded0"), s_("r13_loaded1")]
                r2_loaded = [s_("r2_loaded0"), s_("r2_loaded1")]
                scaled13, scaled2 = s_("scaled13"), s_("scaled2")
                t13_done, t2_done = s_("t13_done"), s_("t2_done")
                t_hi, t_lo = s_("t_hi"), s_("t_lo")
                g_done, u_done, silu_done = s_("g_done"), s_("u_done"), s_("silu")
                h_done, h_hi, h_lo = s_("h_done"), s_("h_hi"), s_("h_lo")
                y_done, y_added, y_stored = s_("y_done"), s_("y_added"), s_("y_stored")
                NP = NI // 2
                NY = 2 * TT
                T13, T2 = 4, 2
                PER = 2 * (T13 + T2)

                def t13_first(p, par):
                    return PER * p + T13 * par

                def t2_first(p, par):
                    return PER * p + 2 * T13 + T2 * par

                with nc.Block() as block:
                    @block.sync
                    def _(sp):
                        for n, s in enumerate((w1_scale, w3_scale)):
                            sp.dma_start(sc13[:, n, :, :].rearrange("p a b -> p (a b)"),
                                         s.rearrange("(o a) b -> o (a b)", o=1).broadcast_to([P, NI * KT])
                                         ).then_inc(sc_loaded, 16)
                        sp.dma_start(sc2[:, :, :].rearrange("p a b -> p (a b)"),
                                     w2_scale.rearrange("(o a) b -> o (a b)", o=1).broadcast_to(
                                         [P, KT * NI])
                                     ).then_inc(sc_loaded, 16)

                        def load13(p, par):
                            rows = bass.ds((2 * p + par) * P, P)
                            for n, w in enumerate((w1, w3)):
                                sp.dma_start(raw13[:, par, n, :], w[rows, :]
                                             ).then_inc(r13_loaded[par], 16)

                        w2_v = w2.rearrange("(n p) (a s i) -> a s p n i", p=P, s=2, i=P)

                        def load2(p, par):
                            sp.dma_start(raw2[:, par, :, :], w2_v[bass.ds(p, 1), par]
                                         .rearrange("a p n i -> (a p) n i")
                                         ).then_inc(r2_loaded[par], 16)
                        for par in range(2):
                            load13(0, par)
                        for par in range(2):
                            load2(0, par)
                        with sp.Fori(0, NP - 1) as p:
                            for par in range(2):
                                sp.wait_ge(t13_done, T13 * (2 * p + par + 1))
                                load13(p + 1, par)
                            for par in range(2):
                                sp.wait_ge(t2_done, T2 * (2 * p + par + 1))
                                load2(p + 1, par)
                        of = out.rearrange("b q n -> (b q) n")
                        for t in range(TT):
                            sp.wait_ge(y_added, NY * (NP - 1) + 2 * (t + 1))
                            tok = half * HALF + t * P
                            sp.dma_start(of[tok:tok + P, :], y[:, t, :]).then_inc(y_stored, 16)
                        sp.wait_ge(y_stored, 16 * TT)

                    @block.gpsimd
                    def _(pool):
                        pool.wait_ge(sc_loaded, 48)

                        def scale13(p, par):
                            pool.wait_ge(r13_loaded[par], 32 * (p + 1))
                            for n in range(2):
                                w = raw13[:, par, n, :].rearrange("p (k c) -> p k c", k=KT)
                                s = sc13[:, n, bass.ds(2 * p + par, 1), :].rearrange(
                                    "p a k -> p (a k)").unsqueeze(2).broadcast_to([P, KT, P])
                                pool.tensor_tensor(w, w, s, ALU.mult).then_inc(scaled13, 1)

                        def scale2(p, par):
                            pool.wait_ge(r2_loaded[par], 16 * (p + 1))
                            w = raw2[:, par, :, :]
                            s = sc2[:, :, bass.ds(2 * p + par, 1)].broadcast_to([P, KT, P])
                            pool.tensor_tensor(w, w, s, ALU.mult).then_inc(scaled2, 1)
                        with pool.Fori(0, NP) as p:
                            for par in range(2):
                                scale13(p, par)
                            for par in range(2):
                                scale2(p, par)

                    def transposed13(par, n):
                        m, kh = n // 2, n % 2
                        return tuple(w[:, par, m, 4 * kh:4 * kh + 4, :].rearrange("p k i -> p (k i)")
                                     for w in (w13_h, w13_l))

                    def transposed2(par, n):
                        return tuple(w[:, par, n * FB:(n + 1) * FB] for w in (w2_h, w2_l))

                    @block.scalar
                    def _(act):
                        def split13(p, par):
                            for n in range(T13):
                                act.wait_ge(t13_done, T13 * (2 * p + par) + n + 1)
                                nc.scalar.activation(transposed13(par, n)[0], t_bank[n % 2][:, :],
                                                     ACT.Copy).then_inc(t_hi, 1)

                        def split2(p, par):
                            for n in range(T2):
                                act.wait_ge(t2_done, T2 * (2 * p + par) + n + 1)
                                nc.scalar.activation(transposed2(par, n)[0], t_bank[n % 2][:, :],
                                                     ACT.Copy).then_inc(t_hi, 1)

                        def gates(p, par, tb):
                            n = 4 * p + 2 * par + tb
                            act.wait_ge(g_done, n + 1)
                            wait(act, h_done, n - 1)
                            nc.scalar.activation(gate[:, tb, :], g_bank[tb][:, 0:TB], ACT.Silu
                                                 ).then_inc(silu_done, 1)
                            act.wait_ge(h_done, n + 1)
                            wait(act, y_done, NY * p)
                            nc.scalar.activation(h_h[:, par, tb * TB:(tb + 1) * TB], hf[:, tb, :],
                                                 ACT.Copy).then_inc(h_hi, 1)
                        split13(0, 0)
                        split13(0, 1)

                        def pair(p, more):
                            split2(p, 0)
                            split2(p, 1)
                            gates(p, 0, 0)
                            gates(p, 0, 1)
                            if more:
                                split13(p + 1, 0)
                            gates(p, 1, 0)
                            gates(p, 1, 1)
                            if more:
                                split13(p + 1, 1)
                        pair(0, True)
                        with act.Fori(1, NP - 1) as p:
                            pair(p, True)
                        pair(NP - 1, False)

                    @block.vector
                    def _(dve):
                        def split13(p, par, banks=range(T13)):
                            for n in banks:
                                hi, lo = transposed13(par, n)
                                dve.wait_ge(t_hi, t13_first(p, par) + n + 1)
                                to_lo(lo, t_bank[n % 2][:, :], hi).then_inc(t_lo, 1)

                        def split2(p, par):
                            for n in range(T2):
                                hi, lo = transposed2(par, n)
                                dve.wait_ge(t_hi, t2_first(p, par) + n + 1)
                                to_lo(lo, t_bank[n % 2][:, :], hi).then_inc(t_lo, 1)

                        def hidden(p, par, tb):
                            n = 4 * p + 2 * par + tb
                            dve.wait_ge(silu_done, n + 1)
                            dve.wait_ge(u_done, n + 1)
                            wait(dve, h_lo, n - 1)
                            nc.vector.tensor_tensor(hf[:, tb, :], u_bank[tb][:, 0:TB],
                                                    gate[:, tb, :], ALU.mult).then_inc(h_done, 1)
                            dve.wait_ge(h_hi, n + 1)
                            cols = slice(tb * TB, (tb + 1) * TB)
                            to_lo(h_l[:, par, cols], hf[:, tb, :], h_h[:, par, cols]
                                  ).then_inc(h_lo, 1)

                        def add_y(p, tiles):
                            for t in tiles:
                                for n in range(2):
                                    dve.wait_ge(y_done, NY * p + 2 * t + n + 1)
                                    cols = slice(n * FB, (n + 1) * FB)
                                    nc.vector.tensor_tensor(y[:, t, cols], y_bank[n][:, :],
                                                            y[:, t, cols], ALU.add
                                                            ).then_inc(y_added, 1)

                        def pair(p, more):
                            split2(p, 0)
                            split2(p, 1)
                            hidden(p, 0, 0)
                            hidden(p, 0, 1)
                            if more:
                                split13(p + 1, 0)
                            hidden(p, 1, 0)
                            hidden(p, 1, 1)
                            for t in range(TT):
                                add_y(p, [t])
                                if more and t < T13:
                                    split13(p + 1, 1, [t])
                        split13(0, 0)
                        split13(0, 1)
                        pair(0, True)
                        with dve.Fori(1, NP - 1) as p:
                            pair(p, True)
                        pair(NP - 1, False)

                    @block.tensor
                    def _(pe):
                        def transpose13(p, par, n):
                            m, kh = n // 2, n % 2
                            pe.wait_ge(scaled13, 2 * (2 * p + par) + m + 1)
                            wait(pe, t_lo, t13_first(p, par) + n - 1)
                            for k in range(4):
                                kk = 4 * kh + k
                                last = pe.transpose(t_bank[n % 2][:, k * P:(k + 1) * P],
                                                    raw13[:, par, m, kk * P:(kk + 1) * P],
                                                    ident[:])
                            last.then_inc(t13_done, 1)

                        def transpose2(p, par, n):
                            pe.wait_ge(scaled2, 2 * p + par + 1)
                            wait(pe, t_lo, t2_first(p, par) + n - 1)
                            for k in range(4):
                                last = pe.transpose(t_bank[n % 2][:, k * P:(k + 1) * P],
                                                    raw2[:, par, 4 * n + k, :], ident[:])
                            last.then_inc(t2_done, 1)

                        def gate_up(p, par, tb, more):
                            n = 4 * p + 2 * par + tb
                            if tb == 0:
                                pe.wait_ge(t_lo, t13_first(p, par) + T13)
                            wait(pe, h_done, n - 1)
                            cols = slice(tb * TB, (tb + 1) * TB)
                            for m, (acc, done) in enumerate(((g_bank, g_done), (u_bank, u_done))):
                                for k in range(KT):
                                    last = split_product(
                                        pe, acc[tb][:, 0:TB],
                                        (w13_h[:, par, m, k, :], w13_l[:, par, m, k, :]),
                                        (x2_h[:, k, cols], x2_l[:, k, cols]), k == 0, k == KT - 1)
                                    if k % 4 == 1 and tb == 0:
                                        n = 2 * m + k // 4
                                        if par == 0:
                                            transpose2(p, n // T2, n % T2)
                                        elif more:
                                            transpose13(p + 1, 0, n)
                                last.then_inc(done, 1)

                        def down(p, t):
                            pe.wait_ge(h_lo, 4 * p + (3 if (t + 1) * P <= TB else 4))
                            for n in range(2):
                                wait(pe, y_added, NY * p + 2 * t + n - 1)
                                rows, cols = slice(t * P, (t + 1) * P), slice(n * FB, (n + 1) * FB)
                                for par in range(2):
                                    last = split_product(
                                        pe, y_bank[n][:, :],
                                        (h_h[:, par, rows], h_l[:, par, rows]),
                                        (w2_h[:, par, cols], w2_l[:, par, cols]),
                                        par == 0, par == 1)
                                last.then_inc(y_done, 1)

                        def pair(p, more):
                            for par in range(2):
                                for tb in range(2):
                                    gate_up(p, par, tb, more)
                            pe.wait_ge(t_lo, t2_first(p, 1) + T2)
                            for t in range(TT):
                                down(p, t)
                                if more and t < T13:
                                    transpose13(p + 1, 1, t)
                        for par in range(2):
                            for n in range(T13):
                                transpose13(0, par, n)
                        pair(0, True)
                        with pe.Fori(1, NP - 1) as p:
                            pair(p, True)
                        pair(NP - 1, False)

        queries()
        attention()
        y = top.enter_context(nc.sbuf_tensor("y", [P, TT, D], f32))
        x2_h = top.enter_context(nc.sbuf_tensor("x2_h", [P, KT, HALF], f32r))
        x2_l = top.enter_context(nc.sbuf_tensor("x2_l", [P, KT, HALF], f32r))
        for half in range(2):
            mixing(half, y, x2_h, x2_l)
            ffn(half, y, x2_h, x2_l)


_INS = ['x', 'ctx_4096', 'L0_xattn_Wq', 'L0_xattn_Wk', 'L0_xattn_Wv', 'L0_xattn_Wo', 'L0_ffn_w1',
        'L0_ffn_w1_scale', 'L0_ffn_w3', 'L0_ffn_w3_scale', 'L0_ffn_w2', 'L0_ffn_w2_scale']


def kernel(**inputs):
    import numpy as _np
    import concourse.bacc as _bacc
    from concourse import mybir as _mybir
    from concourse.bass_utils import run_bass_kernel_spmd as _run

    nc = _bacc.Bacc("TRN2", target_bir_lowering=False, num_devices=1)
    arrays, args = {}, []
    for name in _INS:
        a = _np.ascontiguousarray(inputs[name])
        arrays[f"in_{name}"] = a
        args.append(nc.dram_tensor(f"in_{name}", a.shape, _mybir.dt.from_np(a.dtype),
                                   kind="ExternalInput").ap())
    out = nc.dram_tensor("out", arrays["in_x"].shape, _mybir.dt.float32, kind="ExternalOutput").ap()
    build_program(nc, *args, out)
    r = _run(nc, [arrays], core_ids=[0])
    return r.results[0]["out"]
```

```python
def build_program(nc, x, ctx, wq, wk, wv, wo, w1, w1_scale, w3, w3_scale, w2, w2_scale, out):
    import concourse.bass as bass
    from concourse import mybir
    from contextlib import ExitStack

    f32, f32r = mybir.dt.float32, mybir.dt.float32r
    ALU, AX, ACT = mybir.AluOpType, mybir.AxisListType, mybir.ActivationFunctionType

    P = 128
    B, SQ, D = x.shape
    SK = ctx.shape[1]
    KV = wk.shape[1]
    HD = 32
    NKV = KV // HD
    J = D // KV
    NH = NKV * J
    R = P // HD
    NG = NKV // R
    KT = D // P
    TOK = B * SQ
    GB = 4
    GT = GB * SQ
    CK = 125
    NC = SK // CK
    SKP = SK + 1
    INTER = w1.shape[0]
    NI = INTER // P
    HALF = TOK // 2
    TB = HALF // 2
    TT = HALF // P
    FB = 512
    EPS = 1e-5
    SCALE = HD ** -0.5
    assert NC * CK == SK and TT * P == HALF and GT <= FB and TB <= FB

    q_scr = nc.dram_tensor("q_scratch", [B, 2, P, NG, J * SQ], f32).ap()
    k_scr = nc.dram_tensor("k_scratch", [2, 2, NG, P, SKP], f32).ap()
    a_scr = nc.dram_tensor("attn_scratch", [P, NG * J, TOK], f32).ap()
    wt_scr = nc.dram_tensor("weight_scratch", [NI, 3, P, D], f32).ap()

    top = ExitStack()

    def sem(name):
        return top.enter_context(nc.semaphore(name))

    def split_product(pe, acc, lhs, rhs, first, last):
        (lh, ll), (rh, rl) = lhs, rhs
        pe.matmul(acc, lh, rh, start=first, stop=False)
        pe.matmul(acc, lh, rl, start=False, stop=False)
        return pe.matmul(acc, ll, rh, start=False, stop=last)

    def to_lo(dst, src, hi):
        return nc.vector.tensor_tensor(dst, src, hi.bitcast(f32), ALU.subtract)

    def wait(eng, s, value):
        if not isinstance(value, int) or value > 0:
            eng.wait_ge(s, value)

    with top:
        ident = top.enter_context(nc.sbuf_tensor("ident", [P, P], f32))
        neghalf = top.enter_context(nc.sbuf_tensor("neghalf", [P, 1], f32))
        bank = [top.enter_context(nc.psum_tensor(f"bank{i}", [P, FB], f32)) for i in range(8)]
        hold = top.enter_context(nc.sbuf_tensor("hold", [1, 3], f32))
        consts = sem("consts")
        stash = top.enter_context(nc.sbuf_tensor("stash", [P, 12, D], f32))
        ctx_in = stash[0:CK, 0:2 * NC, :].rearrange("p (s c) n -> p s c n", s=2)
        wkv_raw = stash[:, 8:12, :].rearrange("p a (b n) -> p (a b) n", n=2 * KV)
        wo_raw = stash[:, 0:KT, :]
        attn_in, x_in = stash[:, 8:10, :].rearrange("p s (c q) -> p s c q", q=P), stash[:, 10:12, :]
        raw13 = stash[:, 0:4, :].rearrange("p (s m) n -> p s m n", s=2)
        raw2 = stash[:, 4:6, :].rearrange("p s (n i) -> p s n i", i=P)
        sc13 = stash[:, 6, 0:2 * NI * KT].rearrange("p (m a k) -> p m a k", m=2, k=KT)
        sc2 = stash[:, 6, 2 * NI * KT:3 * NI * KT].rearrange("p (k a) -> p k a", k=KT)
        wkv_loaded = sem("wkv_loaded")
        c_loaded = [sem("c_loaded0"), sem("c_loaded1")]
        wo_loaded = [sem("wo_loaded0"), sem("wo_loaded1")]
        a_loaded = [[sem(f"a_loaded{h}{i}") for i in range(2)] for h in range(2)]
        x_loaded = [[sem(f"x_loaded{h}{i}") for i in range(2)] for h in range(2)]
        sc_loaded = sem("sc_loaded")
        wt_stored = [sem(f"wt_stored{i}") for i in range(3)]
        r13_loaded = [[sem(f"r13_loaded{h}{i}") for i in range(2)] for h in range(2)]
        r2_loaded = [[sem(f"r2_loaded{h}{i}") for i in range(2)] for h in range(2)]
        scaled13 = sem("scaled13")
        y_stored = [sem("y_stored0"), sem("y_stored1")]

        def load_ctx(sp, n, slot):
            for c in range(NC):
                sp.dma_start(ctx_in[:, slot, c, :], ctx[bass.ds(n, 1), c * CK:(c + 1) * CK, :]
                             .rearrange("b k n -> k (b n)")).then_inc(c_loaded[slot], 16)

        def load_wo(sp, half, chunks):
            rows = wo.rearrange("(g r j d) n -> g j r d n", g=NG, r=R, j=J)
            for c in chunks:
                for r in range(R):
                    sp.dma_start(wo_raw[r * HD:(r + 1) * HD, c, :], rows[c // J, c % J, r]
                                 ).then_inc(wo_loaded[half], 16)

        def load_tile(sp, half, t, slot):
            tok = half * HALF + t * P
            sp.dma_start(attn_in[:, slot, :, :], a_scr[:, :, bass.ds(tok, P)]
                         ).then_inc(a_loaded[half][slot], 16)
            sp.dma_start(x_in[:, slot, :], x.rearrange("b q n -> (b q) n")[bass.ds(tok, P), :]
                         ).then_inc(x_loaded[half][slot], 16)

        def load13(sp, half, p, par):
            for n, w in enumerate((w1, w3)):
                src = w[bass.ds((2 * p + par) * P, P), :] if half == 0 else wt_scr[
                    bass.ds(2 * p + par, 1), n].rearrange("a p n -> (a p) n")
                sp.dma_start(raw13[:, par, n, :], src).then_inc(r13_loaded[half][par], 16)

        w2_v = w2.rearrange("(n p) (a s i) -> a s p n i", p=P, s=2, i=P)

        def load2(sp, half, p, par):
            if half == 0:
                dst = raw2[:, par, :, :]
                src = w2_v[bass.ds(p, 1), par].rearrange("a p n i -> (a p) n i")
            else:
                dst = raw2[:, par, :, :].rearrange("p n i -> p (n i)")
                src = wt_scr[bass.ds(2 * p + par, 1), 2].rearrange("a p n -> (a p) n")
            sp.dma_start(dst, src).then_inc(r2_loaded[half][par], 16)

        def load_scales(sp):
            for n, s in enumerate((w1_scale, w3_scale)):
                sp.dma_start(sc13[:, n, :, :].rearrange("p a b -> p (a b)"),
                             s.rearrange("(o a) b -> o (a b)", o=1).broadcast_to([P, NI * KT])
                             ).then_inc(sc_loaded, 16)
            sp.dma_start(sc2[:, :, :].rearrange("p a b -> p (a b)"),
                         w2_scale.rearrange("(o a) b -> o (a b)", o=1).broadcast_to([P, KT * NI])
                         ).then_inc(sc_loaded, 16)

        def scale13(pool, p, par):
            pool.wait_ge(r13_loaded[0][par], 32 * (p + 1))
            for n in range(2):
                w = raw13[:, par, n, :].rearrange("p (k c) -> p k c", k=KT)
                s = sc13[:, n, bass.ds(2 * p + par, 1), :].rearrange(
                    "p a k -> p (a k)").unsqueeze(2).broadcast_to([P, KT, P])
                pool.tensor_tensor(w, w, s, ALU.mult).then_inc(scaled13, 1)

        def queries():
            with ExitStack() as st:
                def sb(name, shape, dt=f32):
                    return st.enter_context(nc.sbuf_tensor("q_" + name, shape, dt))
                wraw = stash[:, 0:KT, :]
                w_h, w_l = sb("w_h", [P, KT, NG * J, P], f32r), sb("w_l", [P, KT, NG * J, P], f32r)
                xin = sb("xin", [SQ, 2, D])
                stats, aggr = sb("stats", [SQ, 2, 6]), sb("aggr", [SQ, 2])
                veps, rstd = sb("veps", [SQ, 1]), sb("rstd", [SQ, 1])
                xn = sb("xn", [SQ, GB, D])
                xT_h, xT_l = sb("xT_h", [P, 2, KT, GT], f32r), sb("xT_l", [P, 2, KT, GT], f32r)
                q_h, q_l = sb("q_h", [P, NG * J, GT], f32r), sb("q_l", [P, NG * J, GT], f32r)
                w_loaded = [[sem(f"q_w_loaded{g}{k}") for k in range(KT)] for g in range(NG)]
                w_hi, w_lo = sem("q_w_hi"), sem("q_w_lo")
                xin_loaded = [sem("q_x_loaded0"), sem("q_x_loaded1")]
                stats_done, aggr_done, veps_done = sem("q_stats"), sem("q_aggr"), sem("q_veps")
                rstd_done, xn_done = sem("q_rstd"), sem("q_xn")
                t_done, xT_hi, xT_lo = sem("q_t_done"), sem("q_xT_hi"), sem("q_xT_lo")
                p_done, p_hi, p_lo = sem("q_p_done"), sem("q_p_hi"), sem("q_p_lo")
                NGRP, C = B // GB, NG * J
                q_stored = [sem(f"q_stored{c}") for c in range(C)]
                assert C == 2 * GB

                def perm(a, g):
                    return a[:, :, g * J * P:(g + 1) * J * P].rearrange(
                        "p k (r j d) -> p k j r d", r=R, j=J)

                def wcols(a, k, g):
                    return a[:, k, g * J:(g + 1) * J, :].rearrange("p j (r d) -> p j r d", r=R)

                def xT_part(a, grp, n):
                    s, kh = n // 2, n % 2
                    return a[:, grp % 2, 4 * kh:4 * kh + 4, s * SQ:(s + 1) * SQ]

                def next_norm(grp, c):
                    t = GB * (grp + 1) + (c + 1) // 2
                    return t if c % 2 and t < B else None

                with nc.Block() as block:
                    @block.sync
                    def _(sp):
                        wv_ = wq.rearrange("(k p) n -> p k n", p=P)

                        def load_x(t):
                            if t >= 2:
                                sp.wait_ge(xn_done, t - 1)
                            sp.dma_start(xin[:, t % 2, :], x[t]).then_inc(xin_loaded[t % 2], 16)

                        def load_w(g, k):
                            cols = slice(g * J * P, (g + 1) * J * P)
                            sp.dma_start(wraw[:, k, cols], wv_[:, k, cols]
                                         ).then_inc(w_loaded[g][k], 16)
                        load_x(0)
                        load_x(1)
                        for k in range(KT):
                            load_w(0, k)
                        for t in range(2, GB + 1):
                            load_x(t)
                        for k in range(KT):
                            load_w(1, k)
                        for n, w in enumerate((wk, wv)):
                            sp.dma_start(wkv_raw[:, :, n * KV:(n + 1) * KV],
                                         w.rearrange("(k p) n -> p k n", p=P)
                                         ).then_inc(wkv_loaded, 16)
                        load_x(GB + 1)
                        load_x(GB + 2)
                        for grp in range(NGRP):
                            for c in range(C):
                                sp.wait_ge(p_lo, C * grp + c + 1)
                                g, cols = c // J, slice(c % J * SQ, (c % J + 1) * SQ)
                                for hl, buf in enumerate((q_h, q_l)):
                                    sp.dma_start(
                                        q_scr[GB * grp:GB * (grp + 1), hl, :, g, cols].rearrange(
                                            "b p q -> p b q"),
                                        buf[:, c, :].bitcast(f32).rearrange("p (b q) -> p b q", q=SQ)
                                        ).then_inc(q_stored[c], 16)
                                t = next_norm(grp, c)
                                if t is not None and t + 2 < B:
                                    load_x(t + 2)
                            if grp == 0:
                                sp.wait_ge(w_lo, KT * NG)
                                load_ctx(sp, 0, 0)
                                load_ctx(sp, 1, 1)
                        for c in range(C):
                            sp.wait_ge(q_stored[c], 32 * NGRP)

                    @block.gpsimd
                    def _(pool):
                        pool.memset(ident[:], 0.0).then_inc(consts, 1)
                        pool.memset(neghalf[:], -0.5).then_inc(consts, 1)
                        pool.wait_ge(consts, 2)
                        pool.affine_select(out=ident[:], in_=ident[:], compare_op=ALU.not_equal,
                                           fill=1.0, base=0, pattern=[[-1, P]],
                                           channel_multiplier=1).then_inc(consts, 1)
                        with pool.Fori(0, B) as t:
                            pool.wait_ge(veps_done, t + 1)
                            pool.tensor_tensor(rstd[:], veps[:], neghalf[0:SQ, :], ALU.pow
                                               ).then_inc(rstd_done, 1)

                    @block.vector
                    def _(dve):
                        def norm(t):
                            slot = t % 2
                            dve.wait_ge(xin_loaded[slot], 16 * (t // 2 + 1))
                            for h in range(2):
                                nc.vector.bn_stats(stats[:, h, :], xin[:, slot, h * FB:(h + 1) * FB]
                                                   ).then_inc(stats_done, 1)
                            dve.wait_ge(stats_done, 2 * t + 2)
                            nc.vector.memset(hold[:, 2:3], 0.0)
                            nc.vector.bn_aggr(aggr[:], stats[:]).then_inc(aggr_done, 1)
                            dve.wait_ge(aggr_done, t + 1)
                            nc.vector.tensor_scalar(veps[:], aggr[:, 1:2], EPS, None, ALU.add
                                                    ).then_inc(veps_done, 1)
                            dve.wait_ge(rstd_done, t + 1)
                            wait(dve, t_done, 2 * (t - GB) + 2)
                            nc.vector.tensor_scalar(xn[:, t % GB, :], xin[:, slot, :], aggr[:, 0:1],
                                                    rstd[:], ALU.subtract, ALU.mult
                                                    ).then_inc(xn_done, 1)

                        def split_w(g, k):
                            dve.wait_ge(w_hi, KT * g + k + 1)
                            to_lo(wcols(w_l, k, g), perm(wraw, g)[:, k], wcols(w_h, k, g)
                                  ).then_inc(w_lo, 1)

                        def split_x(grp, n):
                            dve.wait_ge(xT_hi, 2 * GB * grp + n + 1)
                            to_lo(xT_part(xT_l, grp, n),
                                  bank[n % 2][:, 0:4 * SQ].rearrange("p (k q) -> p k q", k=4),
                                  xT_part(xT_h, grp, n)).then_inc(xT_lo, 1)
                        norm(0)
                        for s in range(GB):
                            norm(s + 1)
                            for n in (2 * s, 2 * s + 1):
                                split_x(0, n)
                                split_w(0, n)
                        for grp in range(NGRP):
                            for c in range(C):
                                dve.wait_ge(p_hi, C * grp + c + 1)
                                to_lo(q_l[:, c, :], bank[2 + c % 2][:, 0:GT], q_h[:, c, :]
                                      ).then_inc(p_lo, 1)
                                if grp + 1 < NGRP:
                                    split_x(grp + 1, c)
                                if grp == 0 and c < KT // 2:
                                    split_w(1, 2 * c)
                                    split_w(1, 2 * c + 1)
                                if next_norm(grp, c) is not None:
                                    norm(next_norm(grp, c))

                    @block.scalar
                    def _(act):
                        def split_w(g, k):
                            act.wait_ge(w_loaded[g][k], 16)
                            nc.scalar.activation(wcols(w_h, k, g), perm(wraw, g)[:, k], ACT.Copy
                                                 ).then_inc(w_hi, 1)

                        def split_x(grp, n):
                            act.wait_ge(t_done, 2 * GB * grp + n + 1)
                            nc.scalar.activation(
                                xT_part(xT_h, grp, n),
                                bank[n % 2][:, 0:4 * SQ].rearrange("p (k q) -> p k q", k=4),
                                ACT.Copy).then_inc(xT_hi, 1)
                        for n in range(2 * GB):
                            split_x(0, n)
                            split_w(0, n)
                        for grp in range(NGRP):
                            for c in range(C):
                                act.wait_ge(p_done, C * grp + c + 1)
                                wait(act, q_stored[c], 32 * grp)
                                nc.scalar.activation(q_h[:, c, :], bank[2 + c % 2][:, 0:GT],
                                                     ACT.Copy).then_inc(p_hi, 1)
                                if grp + 1 < NGRP:
                                    split_x(grp + 1, c)
                                if grp == 0 and c < KT // 2:
                                    split_w(1, 2 * c)
                                    split_w(1, 2 * c + 1)

                    @block.tensor
                    def _(pe):
                        def transposes(grp, n):
                            s, kh = n // 2, n % 2
                            pe.wait_ge(xn_done, GB * grp + s + 1)
                            wait(pe, xT_lo, 2 * GB * grp + n - 1)
                            for k in range(4):
                                kk = 4 * kh + k
                                last = pe.transpose(bank[n % 2][:, k * SQ:(k + 1) * SQ],
                                                    xn[:, s, kk * P:(kk + 1) * P],
                                                    ident[0:SQ, 0:SQ])
                            last.then_inc(t_done, 1)
                        pe.wait_ge(consts, 3)
                        for n in range(2 * GB):
                            transposes(0, n)
                        for grp in range(NGRP):
                            pe.wait_ge(xT_lo, 2 * GB * (grp + 1))
                            for c in range(C):
                                wait(pe, p_lo, C * grp + c - 1)
                                for k in range(KT):
                                    if grp == 0 and c % J == 0:
                                        pe.wait_ge(w_lo, KT * (c // J) + k + 1)
                                    last = split_product(
                                        pe, bank[2 + c % 2][:, 0:GT],
                                        (w_h[:, k, c, :], w_l[:, k, c, :]),
                                        (xT_h[:, grp % 2, k, :], xT_l[:, grp % 2, k, :]),
                                        k == 0, k == KT - 1)
                                last.then_inc(p_done, 1)
                                if grp + 1 < NGRP:
                                    transposes(grp + 1, c)

        def attention():
            with ExitStack() as st:
                def sb(name, shape, dt=f32):
                    return st.enter_context(nc.sbuf_tensor("a_" + name, shape, dt))
                w_h, w_l = sb("w_h", [P, KT, 2 * KV], f32r), sb("w_l", [P, KT, 2 * KV], f32r)
                cT_h, cT_l = sb("cT_h", [P, KT, SKP], f32r), sb("cT_l", [P, KT, SKP], f32r)
                k_h, k_l = sb("k_h", [P, NG, SKP], f32r), sb("k_l", [P, NG, SKP], f32r)
                kst = sb("kst", [98, 2, NKV, SKP], f32r)
                qst = sb("qst", [98, 2, NKV, J * SQ], f32r)
                vnew, v = sb("vnew", [CK, NC, KV]), sb("v", [CK, 2, NC, KV])
                pr = sb("pr", [P, NG, R, NC, J * SQ])
                o, l = sb("o", [P, NG, J * SQ]), sb("l", [P, NG, J * SQ])
                nm = sb("nm", [SQ, 2, NH])
                nm_h, nm_l = sb("nm_h", [NH, SQ], f32r), sb("nm_l", [NH, SQ], f32r)
                ones = sb("ones", [CK, HD])

                s_bank, st_bank, pj_bank = bank[0:2], bank[2:4], bank[4:6]
                o_bank, l_bank = bank[6], bank[7]
                w_hi, w_lo = sem("a_w_hi"), sem("a_w_lo")
                ready = sem("a_consts")
                t_done, t_hi, t_lo = sem("a_t_done"), sem("a_t_hi"), sem("a_t_lo")
                k_done, k_hi, k_lo = sem("a_k_done"), sem("a_k_hi"), sem("a_k_lo")
                v_done, v_out, v_moved = sem("a_v_done"), sem("a_v_out"), sem("a_v_moved")
                k_stored = sem("a_k_stored")
                kq_loaded = [[sem(f"a_kq_loaded{s}{g}") for g in range(NG)] for s in range(2)]
                s_done, max_done = sem("a_s_done"), sem("a_max_done")
                nmT_done, nm_hi, nm_lo = sem("a_nmT_done"), sem("a_nm_hi"), sem("a_nm_lo")
                nm_loaded = [sem("a_nm_loaded0"), sem("a_nm_loaded1")]
                st_done, exp_done, pv_done = sem("a_st_done"), sem("a_exp_done"), sem("a_pv_done")
                o_copied, l_inverted, o_scaled = sem("a_o_copied"), sem("a_l_inv"), sem("a_o_scaled")
                o_stored = [sem(f"a_o_stored{g}") for g in range(NG)]

                NT = 2 * NC
                NU = NG * NC * R

                STEPS, K0, V0, U0 = 32, 7, 15, 5
                HEADS, h0 = [], 0
                for s in range(STEPS):
                    n = (s + 1) % 2 if s < U0 else 2 if s in (8, 11) else 1
                    HEADS.append(range(h0, h0 + n))
                    h0 += n
                assert h0 == NH
                PV = {}
                for g in range(NG):
                    for c in range(NC):
                        at = U0 + R * (NC * g + c + 1) + 1
                        PV[at], PV[at + 1] = (g, c, False), (g, c, True)
                INV = {21: (0, 0), 23: (0, 1), 25: (0, 2), 27: (0, 3),
                       6: (1, 0), 8: (1, 1), 10: (1, 2), 12: (1, 3)}
                def each(eng, body):
                    body(-1, 0, True, False, False)
                    body(-1, 1, True, True, False)
                    body(0, 0, True, True, True)
                    body(0, 1, True, True, True)
                    with eng.Fori(1, B // 2 - 1) as i:
                        body(i, 0, True, True, True)
                        body(i, 1, True, True, True)
                    body(B // 2 - 1, 0, False, True, True)
                    body(B // 2 - 1, 1, False, False, True)

                with nc.Block() as block:
                    @block.sync
                    def _(sp):
                        def store(b, g):
                            sp.wait_ge(o_scaled, NG * b + g + 1)
                            sp.dma_start(a_scr[:, g * J:(g + 1) * J, bass.ds(b * SQ, SQ)],
                                         o[:, g, :].rearrange("p (j q) -> p j q", j=J)
                                         ).then_inc(o_stored[g], 16)

                        def body(i, par, proj, score, attn):
                            b = 2 * i + par
                            pb = b + 2
                            if attn:
                                sp.wait_ge(nm_lo, b + 1)
                                for row, src in ((96, nm_h), (97, nm_l)):
                                    sp.dma_start(qst[row:row + 1, par, :, :].bitcast(f32).rearrange(
                                        "o g (j q) -> o (g j) q", j=J), src[:, :].bitcast(f32)
                                        ).then_inc(nm_loaded[par], 16)
                            if proj and not (isinstance(b, int) and b == -2):
                                load_next = not (isinstance(b, int)) or b + 3 < B
                                if load_next:
                                    sp.wait_ge(t_done, NT * (b + 2))
                                    load_ctx(sp, b + 3, 1 - par)
                            if attn and not (isinstance(b, int) and b == 0):
                                store(b - 1, 1)
                            if isinstance(b, int) and b == B - 2:
                                sp.wait_ge(t_done, NT * B)
                                load_wo(sp, 0, range(KT))
                                sp.wait_ge(w_lo, KT)
                                for g in range(NG):
                                    sp.wait_ge(o_stored[g], 16 * (2 * P // SQ + 1))
                                load_tile(sp, 0, 0, 0)
                                load_tile(sp, 0, 1, 1)
                            if proj:
                                sp.wait_ge(k_lo, NG * (pb + 1))
                                for hl, buf in enumerate((k_h, k_l)):
                                    sp.dma_start(k_scr[par, hl].rearrange("g p n -> p g n"),
                                                 buf[:, :, :].bitcast(f32)).then_inc(k_stored, 16)
                                sp.wait_ge(k_stored, 32 * (pb + 1))
                                for g in range(NG):
                                    if attn and g == NG - 1:
                                        store(b, 0)
                                    wait(sp, st_done, NU * b + NC * R * (g + 1))
                                    heads = slice(g * R, (g + 1) * R)
                                    for m, (khl, qhl) in enumerate(((0, 0), (1, 0), (0, 1))):
                                        rows = slice(m * HD, (m + 1) * HD)
                                        sp.dma_start(kst[rows, par, heads, :].bitcast(f32),
                                                     k_scr[par, khl, g].rearrange(
                                                         "(r d) n -> d r n", r=R)
                                                     ).then_inc(kq_loaded[par][g], 16)
                                        sp.dma_start(qst[rows, par, heads, :].bitcast(f32),
                                                     q_scr[bass.ds(pb, 1), qhl, :, g].rearrange(
                                                         "b (r d) n -> d (b r) n", r=R)
                                                     ).then_inc(kq_loaded[par][g], 16)

                            elif attn:
                                store(b, 0)

                        body(-1, 0, True, False, False)
                        body(-1, 1, True, True, False)
                        body(0, 0, True, True, True)
                        body(0, 1, True, True, True)
                        with sp.Fori(1, B // 2 - 2) as i:
                            body(i, 0, True, True, True)
                            body(i, 1, True, True, True)
                        body(B // 2 - 2, 0, True, True, True)
                        body(B // 2 - 2, 1, True, True, True)
                        body(B // 2 - 1, 0, False, True, True)
                        body(B // 2 - 1, 1, False, False, True)
                        store(B - 1, 1)
                        for g in range(NG):
                            sp.wait_ge(o_stored[g], 16 * B)

                    @block.gpsimd
                    def _(pool):
                        pool.memset(ones[:], 1.0).then_inc(ready, 1)
                        pool.wait_ge(ready, 1)
                        pool.memset(kst[96:98, :, :, :].bitcast(f32).rearrange("p s g n -> p (s g n)"), 1.0
                                    ).then_inc(ready, 1)
                        pool.wait_ge(ready, 2)
                        pool.memset(cT_h[:, :, SK:SKP].bitcast(f32), 0.0).then_inc(ready, 1)
                        pool.memset(cT_l[:, :, SK:SKP].bitcast(f32), 0.0).then_inc(ready, 1)

                        def body(i, par, proj, score, attn):
                            b = 2 * i + par
                            if attn:
                                for g in range(NG):
                                    pool.wait_ge(l_inverted, J * (NG * b + g + 1))
                                    pool.tensor_tensor(o[:, g, :], o[:, g, :], l[:, g, :],
                                                       ALU.mult).then_inc(o_scaled, 1)
                        each(pool, body)

                    @block.vector
                    def _(dve):
                        def invert(b, g, j):
                            dve.wait_ge(o_copied, 2 * (NG * b + g + 1))
                            part = l[:, g, j * SQ:(j + 1) * SQ]
                            nc.vector.reciprocal(part, part).then_inc(l_inverted, 1)

                        def body(i, par, proj, score, attn):
                            b = 2 * i + par
                            sb_, pb = b + 1, b + 2
                            for s in range(STEPS):
                                if proj and s < NT:
                                    c, kh = s // 2, s % 2
                                    dve.wait_ge(t_hi, NT * pb + s + 1)
                                    dst = (slice(None), slice(4 * kh, 4 * kh + 4),
                                           slice(c * CK, (c + 1) * CK))
                                    n = s if s == 0 else s + 1
                                    to_lo(cT_l[dst], pj_bank[n % 2][:, 0:4 * CK].rearrange(
                                        "p (k n) -> p k n", k=4), cT_h[dst]).then_inc(t_lo, 1)
                                if isinstance(b, int) and b == -2 and s < KT:
                                    dve.wait_ge(w_hi, s + 1)
                                    to_lo(w_l[:, s, :], wkv_raw[:, s, :], w_h[:, s, :]
                                          ).then_inc(w_lo, 1)
                                if attn and s == 0:
                                    dve.wait_ge(nmT_done, b + 1)
                                    wait(dve, nm_loaded[1 - par], 32 * (i + par))
                                    nc.vector.tensor_copy(nm_h[:], pj_bank[1][0:NH, 0:SQ]
                                                          ).then_inc(nm_hi, 1)
                                    dve.wait_ge(nm_hi, b + 1)
                                    to_lo(nm_l[:], pj_bank[1][0:NH, 0:SQ], nm_h[:]
                                          ).then_inc(nm_lo, 1)
                                if score:
                                    for h in HEADS[s]:
                                        dve.wait_ge(s_done, NH * sb_ + h + 1)
                                        nc.vector.tensor_reduce(nm[:, 1 - par, h:h + 1],
                                                                s_bank[h % 2][0:SQ, 0:SK], AX.X,
                                                                ALU.max, negate=True
                                                                ).then_inc(max_done, 1)
                                if score and s == 9:
                                    dve.wait_ge(v_out, NC * (sb_ + 1))
                                    wait(dve, pv_done, NG * b)
                                    nc.vector.tensor_copy(v[:, 1 - par, :, :], vnew[:, :, :]
                                                          ).then_inc(v_moved, 1)
                                if proj and s in (K0 + 3, K0 + 7):
                                    g = (s - K0) // 4
                                    dve.wait_ge(k_hi, NG * pb + g + 1)
                                    to_lo(k_l[:, g, :], pj_bank[(7 + g) % 2][:, 0:SKP],
                                          k_h[:, g, :]).then_inc(k_lo, 1)
                                if proj and s in (V0 + 3, V0 + 7, V0 + 11):
                                    c = (s - V0) // 4
                                    dve.wait_ge(v_done, NC * pb + c + 1)
                                    if c == 0:
                                        wait(dve, v_moved, pb)
                                    nc.vector.tensor_copy(vnew[:, c, :],
                                                          pj_bank[(9 + c) % 2][0:CK, 0:KV]
                                                          ).then_inc(v_out, 1)
                                if attn and s in INV:
                                    g, j = INV[s]
                                    if g == 0:
                                        invert(b, 0, j)
                                    elif not (isinstance(b, int) and b == 0):
                                        invert(b - 1, 1, j)
                        each(dve, body)
                        for j in range(J):
                            invert(B - 1, 1, j)

                    @block.scalar
                    def _(act):
                        act.wait_ge(wkv_loaded, 32)

                        def copy_out(b, g):
                            act.wait_ge(pv_done, NG * b + g + 1)
                            wait(act, o_stored[g], 16 * b)
                            nc.scalar.activation(o[:, g, :], o_bank[:, 0:J * SQ], ACT.Copy
                                                 ).then_inc(o_copied, 1)
                            nc.scalar.activation(l[:, g, :], l_bank[:, 0:J * SQ], ACT.Copy
                                                 ).then_inc(o_copied, 1)

                        def body(i, par, proj, score, attn):
                            b = 2 * i + par
                            pb = b + 2
                            for s in range(STEPS):
                                if proj and s < NT:
                                    c, kh = s // 2, s % 2
                                    act.wait_ge(t_done, NT * pb + s + 1)
                                    if s == 0:
                                        wait(act, v_done, NC * pb)
                                    n = s if s == 0 else s + 1
                                    nc.scalar.activation(
                                        cT_h[:, 4 * kh:4 * kh + 4, c * CK:(c + 1) * CK],
                                        pj_bank[n % 2][:, 0:4 * CK].rearrange(
                                            "p (k n) -> p k n", k=4), ACT.Copy).then_inc(t_hi, 1)
                                if isinstance(b, int) and b == -2 and s < KT:
                                    nc.scalar.activation(w_h[:, s, :], wkv_raw[:, s, :], ACT.Copy
                                                         ).then_inc(w_hi, 1)
                                if attn and s == 4 and not (isinstance(b, int) and b == 0):
                                    copy_out(b - 1, 1)
                                if proj and s in (K0 + 3, K0 + 7):
                                    g = (s - K0) // 4
                                    act.wait_ge(k_done, NG * pb + g + 1)
                                    if g == 0:
                                        wait(act, k_stored, 32 * pb)
                                    nc.scalar.activation(k_h[:, g, :],
                                                         pj_bank[(7 + g) % 2][:, 0:SKP], ACT.Copy
                                                         ).then_inc(k_hi, 1)
                                if attn and 0 <= s - U0 < NU:
                                    u = s - U0
                                    g, c, r = u // (NC * R), u // R % NC, u % R
                                    act.wait_ge(st_done, NU * b + u + 1)
                                    if c == 0 and r == 0:
                                        wait(act, pv_done, NG * (b - 1) + g + 1)
                                    nc.scalar.activation(pr[0:CK, g, r, c, :],
                                                         st_bank[u % 2][0:CK, 0:J * SQ], ACT.Exp,
                                                         scale=SCALE).then_inc(exp_done, 1)
                                if attn and s == 20:
                                    copy_out(b, 0)
                        each(act, body)
                        copy_out(B - 1, 1)

                    @block.tensor
                    def _(pe):
                        def body(i, par, proj, score, attn):
                            b = 2 * i + par
                            sb_, pb = b + 1, b + 2
                            for s in range(STEPS):
                                for h in HEADS[s] if score else ():
                                    g, j = h // J, h % J
                                    if h % (NH // NG) == 0:
                                        pe.wait_ge(kq_loaded[1 - par][h * NG // NH],
                                                   96 * (i + par + 1))
                                    wait(pe, max_done, NH * sb_ + h - 1)
                                    pe.matmul(s_bank[h % 2][0:SQ, 0:SKP],
                                              qst[0:96, 1 - par, g, j * SQ:(j + 1) * SQ],
                                              kst[0:96, 1 - par, g, :], start=True, stop=True
                                              ).then_inc(s_done, 1)
                                if proj and s < NT:
                                    c, kh = s // 2, s % 2
                                    if s == 0:
                                        pe.wait_ge(c_loaded[par], 16 * NC * (i + 2))
                                        wait(pe, v_out, NC * pb - 1)
                                    elif s == 2 and attn:
                                        pe.wait_ge(nm_lo, b + 1)
                                    elif s == 2:
                                        wait(pe, v_out, NC * pb)
                                    else:
                                        pe.wait_ge(t_lo, NT * pb + (1 if s == 1 else s - 1))
                                    n = s if s == 0 else s + 1
                                    for k in range(4):
                                        kk = 4 * kh + k
                                        last = pe.transpose(pj_bank[n % 2][:, k * CK:(k + 1) * CK],
                                                            ctx_in[:, par, c, kk * P:(kk + 1) * P],
                                                            ident[0:CK, 0:CK])
                                    last.then_inc(t_done, 1)
                                if attn and s == 0:
                                    pe.wait_ge(max_done, NH * (b + 1))
                                    done = NC * (b + 2)
                                    pe.wait_ge(v_out, min(done, NC * B) if isinstance(done, int)
                                               else done)
                                    pe.transpose(pj_bank[1][0:NH, 0:SQ], nm[:, par, :],
                                                 ident[0:SQ, 0:SQ]).then_inc(nmT_done, 1)
                                if proj and K0 <= s < K0 + 8:
                                    g, k0 = (s - K0) // 4, 2 * ((s - K0) % 4)
                                    if s == K0:
                                        if isinstance(b, int) and b == -2:
                                            pe.wait_ge(w_lo, KT)
                                            pe.wait_ge(ready, 4)
                                        pe.wait_ge(t_lo, NT * (pb + 1))
                                    for k in range(k0, k0 + 2):
                                        last = split_product(
                                            pe, pj_bank[(7 + g) % 2][:, 0:SKP],
                                            (w_h[:, k, g * P:(g + 1) * P], w_l[:, k, g * P:(g + 1) * P]),
                                            (cT_h[:, k, :], cT_l[:, k, :]), k == 0, k == KT - 1)
                                    if k0 == KT - 2:
                                        last.then_inc(k_done, 1)
                                if proj and V0 <= s < V0 + 12:
                                    c, k0 = (s - V0) // 4, 2 * ((s - V0) % 4)
                                    keys = slice(c * CK, (c + 1) * CK)
                                    if k0 == 0:
                                        if c < 2:
                                            pe.wait_ge(k_lo, NG * pb + c + 1)
                                        else:
                                            pe.wait_ge(v_out, NC * pb + 1)
                                    for k in range(k0, k0 + 2):
                                        last = split_product(
                                            pe, pj_bank[(9 + c) % 2][0:CK, 0:KV],
                                            (cT_h[:, k, keys], cT_l[:, k, keys]),
                                            (w_h[:, k, KV:2 * KV], w_l[:, k, KV:2 * KV]),
                                            k == 0, k == KT - 1)
                                    if k0 == KT - 2:
                                        last.then_inc(v_done, 1)
                                if attn and 0 <= s - U0 < NU:
                                    u = s - U0
                                    g, c, r = u // (NC * R), u // R % NC, u % R
                                    if u == 0:
                                        pe.wait_ge(nm_loaded[par], 32 * (i + 1))
                                    wait(pe, exp_done, NU * b + u - 1)
                                    pe.matmul(st_bank[u % 2][0:CK, 0:J * SQ],
                                              kst[0:98, par, g * R + r, c * CK:(c + 1) * CK],
                                              qst[0:98, par, g * R + r, :], start=True, stop=True
                                              ).then_inc(st_done, 1)
                                if attn and s in PV:
                                    g, c, one = PV[s]
                                    if c == 0 and not one:
                                        wait(pe, o_copied, 2 * (NG * b + g))
                                        pe.wait_ge(v_moved, b + 1)
                                    pe.wait_ge(exp_done, NU * b + R * (NC * g + c + 1))
                                    for r in range(R):
                                        h = (g * R + r) * HD
                                        last = pe.matmul(
                                            (l_bank if one else o_bank)[r * HD:(r + 1) * HD,
                                                                        0:J * SQ],
                                            ones[:, :] if one else v[:, par, c, h:h + HD],
                                            pr[0:CK, g, r, c, :], start=c == 0, stop=c == NC - 1)
                                    if one and c == NC - 1:
                                        last.then_inc(pv_done, 1)
                        each(pe, body)

        def mixing(half, y, x2_h, x2_l):
            with ExitStack() as st:
                C = NG * J

                def sb(name, shape, dt=f32):
                    return st.enter_context(nc.sbuf_tensor(f"m{half}_{name}", shape, dt))

                def s_(name):
                    return sem(f"m{half}_{name}")
                w_h, w_l = sb("w_h", [P, C, D], f32r), sb("w_l", [P, C, D], f32r)
                a_h, a_l = sb("a_h", [P, 2, C, P], f32r), sb("a_l", [P, 2, C, P], f32r)
                xn = sb("xn", [P, 2, D])
                stats, aggr = sb("stats", [P, 2, 6]), sb("aggr", [P, 2])
                veps, rstd = sb("veps", [P, 1]), sb("rstd", [P, 1])
                w_hi, w_lo = s_("w_hi"), s_("w_lo")
                a_hi, a_lo = s_("a_hi"), s_("a_lo")
                o_done, y_done = s_("o_done"), s_("y_done")
                stats_done, aggr_done, veps_done = s_("stats"), s_("aggr"), s_("veps")
                rstd_done, xn_done = s_("rstd"), s_("xn")
                t_done, t_hi, t_lo = s_("t_done"), s_("t_hi"), s_("t_lo")
                o_bank, t_bank = bank[0:2], bank[2:4]

                def tiles(eng, step):
                    step(1, 1, 0)
                    with eng.Fori(1, TT // 2) as i:
                        step(2 * i, 0, i)
                        step(2 * i + 1, 1, i)
                    step(TT - 1, 0, TT // 2)

                with nc.Block() as block:
                    @block.sync
                    def _(sp):
                        sp.wait_ge(w_lo, C)
                        if half == 0:
                            load_scales(sp)
                        else:
                            for stored in wt_stored:
                                sp.wait_ge(stored, 16 * NI)
                        for par in range(2):
                            load13(sp, half, 0, par)
                        for par in range(2):
                            load2(sp, half, 0, par)
                        with sp.Fori(0, TT // 2 - 1) as i:
                            for t, slot in ((2 * i + 2, 0), (2 * i + 3, 1)):
                                sp.wait_ge(y_done, 2 * (t - 1))
                                load_tile(sp, half, t, slot)
                        sp.wait_ge(y_done, 2 * (TT - 2))
                        load_tile(sp, half, TT - 1, 0)

                    @block.gpsimd
                    def _(pool):
                        def inverse_deviations(first, last):
                            with pool.Fori(first, last) as t:
                                pool.wait_ge(veps_done, t + 1)
                                pool.tensor_tensor(rstd[:], veps[:], neghalf[:], ALU.pow
                                                   ).then_inc(rstd_done, 1)
                        inverse_deviations(0, TT // 2)
                        if half == 0:
                            pool.wait_ge(sc_loaded, 48)
                            for par in range(2):
                                scale13(pool, 0, par)
                        inverse_deviations(TT // 2, TT)

                    @block.scalar
                    def _(act):
                        def split_attention(t, slot, use):
                            act.wait_ge(a_loaded[half][slot], 16 * (use + 1))
                            wait(act, o_done, 2 * (t - 1))
                            nc.scalar.activation(a_h[:, slot, :, :], attn_in[:, slot, :, :], ACT.Copy
                                                 ).then_inc(a_hi, 1)

                        def split_x(t):
                            for kh in range(2):
                                act.wait_ge(t_done, 2 * t + kh + 1)
                                nc.scalar.activation(
                                    x2_h[:, 4 * kh:4 * kh + 4, bass.ds(t * P, P)],
                                    t_bank[kh][:, :].rearrange("p (k q) -> p k q", k=4), ACT.Copy
                                ).then_inc(t_hi, 1)
                        split_attention(0, 0, 0)
                        act.wait_ge(wo_loaded[half], 16 * R * C)
                        for c in range(C):
                            nc.scalar.activation(w_h[:, c, :], wo_raw[:, c, :], ACT.Copy
                                                 ).then_inc(w_hi, 1)
                        split_attention(1, 1, 0)

                        def step(t, slot, use):
                            if not (isinstance(t, int) and t == TT - 1):
                                split_attention(t + 1, 1 - slot, use + slot)
                            split_x(t - 1)
                        tiles(act, step)
                        split_x(TT - 1)

                    @block.vector
                    def _(dve):
                        def split_attention(t, slot):
                            dve.wait_ge(a_hi, t + 1)
                            to_lo(a_l[:, slot, :, :], attn_in[:, slot, :, :], a_h[:, slot, :, :]
                                  ).then_inc(a_lo, 1)

                        def residual_norm(t, slot, use):
                            dve.wait_ge(x_loaded[half][slot], 16 * (use + 1))
                            for n in range(2):
                                cols = slice(n * FB, (n + 1) * FB)
                                dve.wait_ge(o_done, 2 * t + n + 1)
                                nc.vector.tensor_tensor(y[:, bass.ds(t, 1), cols].rearrange(
                                    "p t n -> p (t n)"), o_bank[n][:, :],
                                    x_in[:, slot, cols], ALU.add).then_inc(y_done, 1)
                            for n in range(2):
                                cols = slice(n * FB, (n + 1) * FB)
                                dve.wait_ge(y_done, 2 * t + n + 1)
                                nc.vector.memset(hold[:, n:n + 1], 0.0)
                                nc.vector.bn_stats(stats[:, n, :], y[:, bass.ds(t, 1), cols].rearrange(
                                    "p t n -> p (t n)")).then_inc(stats_done, 1)
                            dve.wait_ge(stats_done, 2 * t + 2)
                            nc.vector.memset(hold[:, 2:3], 0.0)
                            nc.vector.bn_aggr(aggr[:], stats[:]).then_inc(aggr_done, 1)
                            dve.wait_ge(aggr_done, t + 1)
                            nc.vector.tensor_scalar(veps[:], aggr[:, 1:2], EPS, None, ALU.add
                                                    ).then_inc(veps_done, 1)
                            dve.wait_ge(rstd_done, t + 1)
                            wait(dve, t_done, 2 * (t - 1))
                            nc.vector.tensor_scalar(xn[:, slot, :], y[:, bass.ds(t, 1), :].rearrange(
                                "p t n -> p (t n)"), aggr[:, 0:1], rstd[:], ALU.subtract, ALU.mult
                                ).then_inc(xn_done, 1)

                        def split_x(t):
                            for kh in range(2):
                                dst = (slice(None), slice(4 * kh, 4 * kh + 4), bass.ds(t * P, P))
                                dve.wait_ge(t_hi, 2 * t + kh + 1)
                                to_lo(x2_l[dst], t_bank[kh][:, :].rearrange(
                                    "p (k q) -> p k q", k=4), x2_h[dst]).then_inc(t_lo, 1)
                        split_attention(0, 0)
                        for c in range(C):
                            dve.wait_ge(w_hi, c + 1)
                            to_lo(w_l[:, c, :], wo_raw[:, c, :], w_h[:, c, :]).then_inc(w_lo, 1)
                        split_attention(1, 1)
                        if half:
                            dve.wait_ge(y_stored[0], 16 * TT)
                        residual_norm(0, 0, 0)

                        def step(t, slot, use):
                            if not (isinstance(t, int) and t == TT - 1):
                                split_attention(t + 1, 1 - slot)
                            residual_norm(t, slot, use)
                            split_x(t - 1)
                        tiles(dve, step)
                        split_x(TT - 1)

                    @block.tensor
                    def _(pe):
                        def product(slot, n, c):
                            cols = slice(n * FB, (n + 1) * FB)
                            return split_product(
                                pe, o_bank[n][:, :], (a_h[:, slot, c, :], a_l[:, slot, c, :]),
                                (w_h[:, c, cols], w_l[:, c, cols]), c == 0, c == C - 1)

                        def products(t, slot):
                            pe.wait_ge(a_lo, t + 1)
                            for n in range(2):
                                pe.wait_ge(y_done, 2 * t + n - 1)
                                for c in range(C):
                                    last = product(slot, n, c)
                                last.then_inc(o_done, 1)

                        def transposes(t, slot):
                            pe.wait_ge(xn_done, t + 1)
                            for kh in range(2):
                                wait(pe, t_lo, 2 * t + kh - 1)
                                for k in range(4):
                                    kk = 4 * kh + k
                                    last = pe.transpose(t_bank[kh][:, k * P:(k + 1) * P],
                                                        xn[:, slot, kk * P:(kk + 1) * P], ident[:])
                                last.then_inc(t_done, 1)
                        pe.wait_ge(a_lo, 1)
                        for c in range(C):
                            pe.wait_ge(w_lo, c + 1)
                            for n in range(2):
                                last = product(0, n, c)
                                if c == C - 1:
                                    last.then_inc(o_done, 1)

                        def step(t, slot, use):
                            products(t, slot)
                            transposes(t - 1, 1 - slot)
                        tiles(pe, step)
                        transposes(TT - 1, 0)

        def ffn(half, y, x2_h, x2_l):
            with ExitStack() as st:
                def sb(name, shape, dt=f32):
                    return st.enter_context(nc.sbuf_tensor(f"f{half}_{name}", shape, dt))

                def s_(name):
                    return sem(f"f{half}_{name}")
                w13_h = sb("w13_h", [P, 2, 2, KT, P], f32r)
                w13_l = sb("w13_l", [P, 2, 2, KT, P], f32r)
                w2_h, w2_l = sb("w2_h", [P, 2, D], f32r), sb("w2_l", [P, 2, D], f32r)
                if half == 0:
                    wt = sb("wt", [P, 3, D])
                gate, hf = sb("gate", [P, 2, TB]), sb("hf", [P, 2, TB])
                h_h, h_l = sb("h_h", [P, 2, HALF], f32r), sb("h_l", [P, 2, HALF], f32r)
                g_bank, u_bank, y_bank, t_bank = bank[0:2], bank[2:4], bank[4:6], bank[6:8]
                scaled2 = s_("scaled2")
                t13_done, t2_done = s_("t13_done"), s_("t2_done")
                t_hi, t_lo = s_("t_hi"), s_("t_lo")
                g_done, u_done, silu_done = s_("g_done"), s_("u_done"), s_("silu")
                h_done, h_hi, h_lo = s_("h_done"), s_("h_hi"), s_("h_lo")
                y_done, y_added = s_("y_done"), s_("y_added")
                NP = NI // 2
                NY = 2 * TT
                T13, T2 = 4, 2
                PER = 2 * (T13 + T2)

                def t13_first(p, par):
                    return PER * p + T13 * par

                def t2_first(p, par):
                    return PER * p + 2 * T13 + T2 * par

                with nc.Block() as block:
                    @block.sync
                    def _(sp):
                        if half == 0:
                            for t in range(2):
                                load_tile(sp, 1, t, t)
                        def store_wt(first_bank, slot, chunk, m):
                            sp.wait_ge(t_hi, first_bank + 2)
                            sp.dma_start(wt_scr[bass.ds(chunk, 1), m].rearrange("a p n -> (a p) n"),
                                         wt[:, slot, :]).then_inc(wt_stored[slot], 16)

                        def store_wt13(p, par):
                            for m in range(2):
                                store_wt(t13_first(p, par) + 2 * m, (2 * par + m) % 3,
                                         2 * p + par, m)

                        def store_wt2(p, par):
                            store_wt(t2_first(p, par), (4 + par) % 3, 2 * p + par, 2)

                        if half == 0:
                            for par in range(2):
                                store_wt13(0, par)
                            with sp.Fori(0, NP - 1) as p:
                                for par in range(2):
                                    sp.wait_ge(t13_done, T13 * (2 * p + par + 1))
                                    load13(sp, half, p + 1, par)
                                for par in range(2):
                                    sp.wait_ge(t2_done, T2 * (2 * p + par + 1))
                                    load2(sp, half, p + 1, par)
                                    store_wt2(p, par)
                                for par in range(2):
                                    store_wt13(p + 1, par)
                            load_wo(sp, 1, range(4))
                            for par in range(2):
                                store_wt2(NP - 1, par)
                            load_wo(sp, 1, range(4, KT))
                        else:
                            with sp.Fori(0, NP - 1) as p:
                                for par in range(2):
                                    sp.wait_ge(t_lo, t13_first(p, par) + T13)
                                    load13(sp, half, p + 1, par)
                                for par in range(2):
                                    sp.wait_ge(t_lo, t2_first(p, par) + T2)
                                    load2(sp, half, p + 1, par)
                        of = out.rearrange("b q n -> (b q) n")
                        for t in range(TT):
                            sp.wait_ge(y_added, NY * (NP - 1) + 2 * (t + 1))
                            tok = half * HALF + t * P
                            sp.dma_start(of[tok:tok + P, :], y[:, t, :]).then_inc(y_stored[half], 16)
                        if half == 1:
                            for h in range(2):
                                sp.wait_ge(y_stored[h], 16 * TT)

                    @block.gpsimd
                    def _(pool):
                        def scale2(p, par):
                            pool.wait_ge(r2_loaded[0][par], 16 * (p + 1))
                            w = raw2[:, par, :, :]
                            s = sc2[:, :, bass.ds(2 * p + par, 1)].broadcast_to([P, KT, P])
                            pool.tensor_tensor(w, w, s, ALU.mult).then_inc(scaled2, 1)
                        if half == 0:
                            for par in range(2):
                                scale2(0, par)
                            with pool.Fori(1, NP) as p:
                                for par in range(2):
                                    scale13(pool, p, par)
                                for par in range(2):
                                    scale2(p, par)

                    def transposed13(par, n):
                        m, kh = n // 2, n % 2
                        return tuple(w[:, par, m, 4 * kh:4 * kh + 4, :].rearrange("p k i -> p (k i)")
                                     for w in (w13_h, w13_l))

                    def transposed2(par, n):
                        return tuple(w[:, par, n * FB:(n + 1) * FB] for w in (w2_h, w2_l))

                    def source13(par, n):
                        return t_bank[n % 2][:, :] if half == 0 else raw13[
                            :, par, n // 2, n % 2 * FB:(n % 2 + 1) * FB]

                    def source2(par, n):
                        return t_bank[n % 2][:, :] if half == 0 else raw2[
                            :, par, 4 * n:4 * n + 4, :].rearrange("p n i -> p (n i)")

                    @block.scalar
                    def _(act):
                        def copy_bank(n, slot, reused):
                            if n % 2 == 0:
                                wait(act, wt_stored[slot], 16 * reused)
                            nc.scalar.activation(wt[:, slot, n % 2 * FB:(n % 2 + 1) * FB],
                                                 t_bank[n % 2][:, :], ACT.Copy)

                        def split13(p, par):
                            if half == 1:
                                act.wait_ge(r13_loaded[1][par], 32 * (p + 1))
                                wait(act, u_done, 4 * (p - 1) + 2 * par + 2)
                            for n in range(T13):
                                if half == 0:
                                    act.wait_ge(t13_done, T13 * (2 * p + par) + n + 1)
                                    unit = 2 * par + n // 2
                                    copy_bank(n, unit % 3, 2 * p + unit // 3)
                                nc.scalar.activation(transposed13(par, n)[0], source13(par, n),
                                                     ACT.Copy).then_inc(t_hi, 1)

                        def split2(p, par):
                            if half == 1:
                                act.wait_ge(r2_loaded[1][par], 16 * (p + 1))
                                wait(act, y_done, NY * p)
                            for n in range(T2):
                                if half == 0:
                                    act.wait_ge(t2_done, T2 * (2 * p + par) + n + 1)
                                    unit = 4 + par
                                    copy_bank(n, unit % 3, 2 * p + unit // 3)
                                nc.scalar.activation(transposed2(par, n)[0], source2(par, n),
                                                     ACT.Copy).then_inc(t_hi, 1)

                        def gates(p, par, tb):
                            n = 4 * p + 2 * par + tb
                            act.wait_ge(g_done, n + 1)
                            wait(act, h_done, n - 1)
                            nc.scalar.activation(gate[:, tb, :], g_bank[tb][:, 0:TB], ACT.Silu
                                                 ).then_inc(silu_done, 1)
                            act.wait_ge(h_done, n + 1)
                            wait(act, y_done, NY * p)
                            nc.scalar.activation(h_h[:, par, tb * TB:(tb + 1) * TB], hf[:, tb, :],
                                                 ACT.Copy).then_inc(h_hi, 1)
                        split13(0, 0)
                        split13(0, 1)

                        def pair(p, more):
                            if isinstance(p, int) and p == 0:
                                gates(p, 0, 0)
                            split2(p, 0)
                            split2(p, 1)
                            if not (isinstance(p, int) and p == 0):
                                gates(p, 0, 0)
                            gates(p, 0, 1)
                            if more:
                                split13(p + 1, 0)
                            gates(p, 1, 0)
                            gates(p, 1, 1)
                            if more:
                                split13(p + 1, 1)
                        pair(0, True)
                        with act.Fori(1, NP - 1) as p:
                            pair(p, True)
                        pair(NP - 1, False)

                    @block.vector
                    def _(dve):
                        def split13(p, par, banks=range(T13)):
                            for n in banks:
                                hi, lo = transposed13(par, n)
                                dve.wait_ge(t_hi, t13_first(p, par) + n + 1)
                                to_lo(lo, source13(par, n), hi).then_inc(t_lo, 1)

                        def split2(p, par):
                            for n in range(T2):
                                hi, lo = transposed2(par, n)
                                dve.wait_ge(t_hi, t2_first(p, par) + n + 1)
                                to_lo(lo, source2(par, n), hi).then_inc(t_lo, 1)

                        def hidden(p, par, tb):
                            n = 4 * p + 2 * par + tb
                            dve.wait_ge(silu_done, n + 1)
                            dve.wait_ge(u_done, n + 1)
                            wait(dve, h_lo, n - 1)
                            nc.vector.tensor_tensor(hf[:, tb, :], u_bank[tb][:, 0:TB],
                                                    gate[:, tb, :], ALU.mult).then_inc(h_done, 1)
                            dve.wait_ge(h_hi, n + 1)
                            cols = slice(tb * TB, (tb + 1) * TB)
                            to_lo(h_l[:, par, cols], hf[:, tb, :], h_h[:, par, cols]
                                  ).then_inc(h_lo, 1)

                        def add_y(p, tiles):
                            for t in tiles:
                                for n in range(2):
                                    dve.wait_ge(y_done, NY * p + 2 * t + n + 1)
                                    cols = slice(n * FB, (n + 1) * FB)
                                    nc.vector.tensor_tensor(y[:, t, cols], y_bank[n][:, :],
                                                            y[:, t, cols], ALU.add
                                                            ).then_inc(y_added, 1)

                        def pair(p, more):
                            if isinstance(p, int) and p == 0:
                                hidden(p, 0, 0)
                            split2(p, 0)
                            split2(p, 1)
                            if not (isinstance(p, int) and p == 0):
                                hidden(p, 0, 0)
                            hidden(p, 0, 1)
                            if more:
                                split13(p + 1, 0)
                            hidden(p, 1, 0)
                            hidden(p, 1, 1)
                            for t in range(TT):
                                add_y(p, [t])
                                if more and t < T13:
                                    split13(p + 1, 1, [t])
                        split13(0, 0)
                        split13(0, 1)
                        pair(0, True)
                        with dve.Fori(1, NP - 1) as p:
                            pair(p, True)
                        pair(NP - 1, False)

                    @block.tensor
                    def _(pe):
                        def transpose13(p, par, n):
                            m, kh = n // 2, n % 2
                            pe.wait_ge(scaled13, 2 * (2 * p + par) + m + 1)
                            wait(pe, t_lo, t13_first(p, par) + n - 1)
                            for k in range(4):
                                kk = 4 * kh + k
                                last = pe.transpose(t_bank[n % 2][:, k * P:(k + 1) * P],
                                                    raw13[:, par, m, kk * P:(kk + 1) * P],
                                                    ident[:])
                            last.then_inc(t13_done, 1)

                        def transpose2(p, par, n):
                            pe.wait_ge(scaled2, 2 * p + par + 1)
                            wait(pe, t_lo, t2_first(p, par) + n - 1)
                            for k in range(4):
                                last = pe.transpose(t_bank[n % 2][:, k * P:(k + 1) * P],
                                                    raw2[:, par, 4 * n + k, :], ident[:])
                            last.then_inc(t2_done, 1)

                        def gate_up(p, par, tb, more):
                            n = 4 * p + 2 * par + tb
                            if tb == 0:
                                pe.wait_ge(t_lo, t13_first(p, par) + T13)
                            wait(pe, h_done, n - 1)
                            cols = slice(tb * TB, (tb + 1) * TB)
                            for m, (acc, done) in enumerate(((g_bank, g_done), (u_bank, u_done))):
                                for k in range(KT):
                                    last = split_product(
                                        pe, acc[tb][:, 0:TB],
                                        (w13_h[:, par, m, k, :], w13_l[:, par, m, k, :]),
                                        (x2_h[:, k, cols], x2_l[:, k, cols]), k == 0, k == KT - 1)
                                    if k % 4 == 1 and half == 0:
                                        n, start = 2 * m + k // 4, isinstance(p, int) and p == 0
                                        if par == 0 and tb == 0 and start:
                                            transpose13(0, 1, n)
                                        elif par == 0 and tb == (1 if start else 0):
                                            transpose2(p, n // T2, n % T2)
                                        elif par == 1 and tb == 0 and more:
                                            transpose13(p + 1, 0, n)
                                last.then_inc(done, 1)

                        def down(p, t):
                            pe.wait_ge(h_lo, 4 * p + (3 if (t + 1) * P <= TB else 4))
                            for n in range(2):
                                wait(pe, y_added, NY * p + 2 * t + n - 1)
                                rows, cols = slice(t * P, (t + 1) * P), slice(n * FB, (n + 1) * FB)
                                for par in range(2):
                                    last = split_product(
                                        pe, y_bank[n][:, :],
                                        (h_h[:, par, rows], h_l[:, par, rows]),
                                        (w2_h[:, par, cols], w2_l[:, par, cols]),
                                        par == 0, par == 1)
                                last.then_inc(y_done, 1)

                        def pair(p, more):
                            for par in range(2):
                                for tb in range(2):
                                    gate_up(p, par, tb, more)
                            pe.wait_ge(t_lo, t2_first(p, 1) + T2)
                            for t in range(TT):
                                down(p, t)
                                if more and t < T13 and half == 0:
                                    transpose13(p + 1, 1, t)
                        if half == 0:
                            for n in range(T13):
                                transpose13(0, 0, n)
                        pair(0, True)
                        with pe.Fori(1, NP - 1) as p:
                            pair(p, True)
                        pair(NP - 1, False)

        queries()
        attention()
        y = top.enter_context(nc.sbuf_tensor("y", [P, TT, D], f32))
        x2_h = top.enter_context(nc.sbuf_tensor("x2_h", [P, KT, HALF], f32r))
        x2_l = top.enter_context(nc.sbuf_tensor("x2_l", [P, KT, HALF], f32r))
        for half in range(2):
            mixing(half, y, x2_h, x2_l)
            ffn(half, y, x2_h, x2_l)


_INS = ['x', 'ctx_4096', 'L0_xattn_Wq', 'L0_xattn_Wk', 'L0_xattn_Wv', 'L0_xattn_Wo', 'L0_ffn_w1',
        'L0_ffn_w1_scale', 'L0_ffn_w3', 'L0_ffn_w3_scale', 'L0_ffn_w2', 'L0_ffn_w2_scale']


def kernel(**inputs):
    import numpy as _np
    import concourse.bacc as _bacc
    from concourse import mybir as _mybir
    from concourse.bass_utils import run_bass_kernel_spmd as _run

    nc = _bacc.Bacc("TRN2", target_bir_lowering=False, num_devices=1,
                     dynamic_dma_scratch_size=1024)
    arrays, args = {}, []
    for name in _INS:
        a = _np.ascontiguousarray(inputs[name])
        arrays[f"in_{name}"] = a
        args.append(nc.dram_tensor(f"in_{name}", a.shape, _mybir.dt.from_np(a.dtype),
                                   kind="ExternalInput").ap())
    out = nc.dram_tensor("out", arrays["in_x"].shape, _mybir.dt.float32, kind="ExternalOutput").ap()
    build_program(nc, *args, out)
    r = _run(nc, [arrays], core_ids=[0])
    return r.results[0]["out"]
```

```python
def build_program(nc, x, ctx, wq, wk, wv, wo, w1, w1_scale, w3, w3_scale, w2, w2_scale, out):
    import concourse.bass as bass
    from concourse import mybir
    from contextlib import ExitStack

    f32, f32r = mybir.dt.float32, mybir.dt.float32r
    ALU, AX, ACT = mybir.AluOpType, mybir.AxisListType, mybir.ActivationFunctionType

    P = 128
    B, SQ, D = x.shape
    SK = ctx.shape[1]
    KV = wk.shape[1]
    HD = 32
    NKV = KV // HD
    J = D // KV
    NH = NKV * J
    R = P // HD
    NG = NKV // R
    KT = D // P
    TOK = B * SQ
    GB = 4
    GT = GB * SQ
    CK = 125
    NC = SK // CK
    SKP = SK + 1
    INTER = w1.shape[0]
    NI = INTER // P
    HALF = TOK // 2
    TB = HALF // 2
    TT = HALF // P
    FB = 512
    EPS = 1e-5
    SCALE = HD ** -0.5
    assert NC * CK == SK and TT * P == HALF and GT <= FB and TB <= FB

    q_scr = nc.dram_tensor("q_scratch", [B, 2, P, NG, J * SQ], f32).ap()
    k_scr = nc.dram_tensor("k_scratch", [2, 2, NG, P, SKP], f32).ap()
    a_scr = nc.dram_tensor("attn_scratch", [P, NG * J, TOK], f32).ap()
    wt_scr = nc.dram_tensor("weight_scratch", [NI, 3, P, D], f32).ap()

    top = ExitStack()

    def sem(name):
        return top.enter_context(nc.semaphore(name))

    def split_product(pe, acc, lhs, rhs, first, last):
        (lh, ll), (rh, rl) = lhs, rhs
        pe.matmul(acc, lh, rh, start=first, stop=False)
        pe.matmul(acc, lh, rl, start=False, stop=False)
        return pe.matmul(acc, ll, rh, start=False, stop=last)

    def to_lo(dst, src, hi):
        return nc.vector.tensor_tensor(dst, src, hi.bitcast(f32), ALU.subtract)

    def wait(eng, s, value):
        if not isinstance(value, int) or value > 0:
            eng.wait_ge(s, value)

    with top:
        ident = top.enter_context(nc.sbuf_tensor("ident", [P, P], f32))
        neghalf = top.enter_context(nc.sbuf_tensor("neghalf", [P, 1], f32))
        bank = [top.enter_context(nc.psum_tensor(f"bank{i}", [P, FB], f32)) for i in range(8)]
        hold = top.enter_context(nc.sbuf_tensor("hold", [1, 3], f32))
        consts = sem("consts")
        stash = top.enter_context(nc.sbuf_tensor("stash", [P, 12, D], f32))
        ctx_in = stash[0:CK, 0:2 * NC, :].rearrange("p (s c) n -> p s c n", s=2)
        wkv_raw = stash[:, 8:12, :].rearrange("p a (b n) -> p (a b) n", n=2 * KV)
        wo_raw = stash[:, 0:KT, :]
        attn_in, x_in = stash[:, 8:10, :].rearrange("p s (c q) -> p s c q", q=P), stash[:, 10:12, :]
        raw13 = stash[:, 0:4, :].rearrange("p (s m) n -> p s m n", s=2)
        raw2 = stash[:, 4:6, :].rearrange("p s (n i) -> p s n i", i=P)
        sc13 = stash[:, 6, 0:2 * NI * KT].rearrange("p (m a k) -> p m a k", m=2, k=KT)
        sc2 = stash[:, 6, 2 * NI * KT:3 * NI * KT].rearrange("p (k a) -> p k a", k=KT)
        wkv_loaded = sem("wkv_loaded")
        c_loaded = [sem("c_loaded0"), sem("c_loaded1")]
        wo_loaded = [sem("wo_loaded0"), sem("wo_loaded1")]
        a_loaded = [[sem(f"a_loaded{h}{i}") for i in range(2)] for h in range(2)]
        x_loaded = [[sem(f"x_loaded{h}{i}") for i in range(2)] for h in range(2)]
        sc_loaded = sem("sc_loaded")
        wt_stored = [sem(f"wt_stored{i}") for i in range(3)]
        r13_loaded = [[sem(f"r13_loaded{h}{i}") for i in range(2)] for h in range(2)]
        r2_loaded = [[sem(f"r2_loaded{h}{i}") for i in range(2)] for h in range(2)]
        scaled13 = sem("scaled13")
        q_stored = [sem(f"q_stored{c}") for c in range(NG * J)]
        o_stored = [sem(f"o_stored{g}") for g in range(NG)]
        y_stored = [sem("y_stored0"), sem("y_stored1")]

        def load_ctx(sp, n, slot):
            for c in range(NC):
                sp.dma_start(ctx_in[:, slot, c, :], ctx[bass.ds(n, 1), c * CK:(c + 1) * CK, :]
                             .rearrange("b k n -> k (b n)")).then_inc(c_loaded[slot], 16)

        def load_wo(sp, half, chunks):
            rows = wo.rearrange("(g r j d) n -> g j r d n", g=NG, r=R, j=J)
            for c in chunks:
                for r in range(R):
                    sp.dma_start(wo_raw[r * HD:(r + 1) * HD, c, :], rows[c // J, c % J, r]
                                 ).then_inc(wo_loaded[half], 16)

        def load_tile(sp, half, t, slot):
            tok = half * HALF + t * P
            sp.dma_start(attn_in[:, slot, :, :], a_scr[:, :, bass.ds(tok, P)]
                         ).then_inc(a_loaded[half][slot], 16)
            sp.dma_start(x_in[:, slot, :], x.rearrange("b q n -> (b q) n")[bass.ds(tok, P), :]
                         ).then_inc(x_loaded[half][slot], 16)

        def load13(sp, half, p, par):
            for n, w in enumerate((w1, w3)):
                src = w[bass.ds((2 * p + par) * P, P), :] if half == 0 else wt_scr[
                    bass.ds(2 * p + par, 1), n].rearrange("a p n -> (a p) n")
                sp.dma_start(raw13[:, par, n, :], src).then_inc(r13_loaded[half][par], 16)

        w2_v = w2.rearrange("(n p) (a s i) -> a s p n i", p=P, s=2, i=P)

        def load2(sp, half, p, par):
            if half == 0:
                dst = raw2[:, par, :, :]
                src = w2_v[bass.ds(p, 1), par].rearrange("a p n i -> (a p) n i")
            else:
                dst = raw2[:, par, :, :].rearrange("p n i -> p (n i)")
                src = wt_scr[bass.ds(2 * p + par, 1), 2].rearrange("a p n -> (a p) n")
            sp.dma_start(dst, src).then_inc(r2_loaded[half][par], 16)

        def load_scales(sp):
            for n, s in enumerate((w1_scale, w3_scale)):
                sp.dma_start(sc13[:, n, :, :].rearrange("p a b -> p (a b)"),
                             s.rearrange("(o a) b -> o (a b)", o=1).broadcast_to([P, NI * KT])
                             ).then_inc(sc_loaded, 16)
            sp.dma_start(sc2[:, :, :].rearrange("p a b -> p (a b)"),
                         w2_scale.rearrange("(o a) b -> o (a b)", o=1).broadcast_to([P, KT * NI])
                         ).then_inc(sc_loaded, 16)

        def scale13(pool, p, par):
            pool.wait_ge(r13_loaded[0][par], 32 * (p + 1))
            for n in range(2):
                w = raw13[:, par, n, :].rearrange("p (k c) -> p k c", k=KT)
                s = sc13[:, n, bass.ds(2 * p + par, 1), :].rearrange(
                    "p a k -> p (a k)").unsqueeze(2).broadcast_to([P, KT, P])
                pool.tensor_tensor(w, w, s, ALU.mult).then_inc(scaled13, 1)

        def queries():
            with ExitStack() as st:
                def sb(name, shape, dt=f32):
                    return st.enter_context(nc.sbuf_tensor("q_" + name, shape, dt))
                wraw = stash[:, 0:KT, :]
                w_h, w_l = sb("w_h", [P, KT, NG * J, P], f32r), sb("w_l", [P, KT, NG * J, P], f32r)
                xn = sb("xn", [SQ, GB, D])
                stats, aggr = sb("stats", [SQ, 2, 6]), sb("aggr", [SQ, 2, 2])
                veps, rstd = sb("veps", [SQ, 2]), sb("rstd", [SQ, 2])
                xT_h, xT_l = sb("xT_h", [P, 2, KT, GT], f32r), sb("xT_l", [P, 2, KT, GT], f32r)
                q_h, q_l = sb("q_h", [P, NG * J, GT], f32r), sb("q_l", [P, NG * J, GT], f32r)
                w_loaded = [sem(f"q_w_loaded{k}") for k in range(KT)] + [sem("q_w_rest_loaded")]
                w_hi, w_lo = sem("q_w_hi"), sem("q_w_lo")
                xin_loaded = [sem(f"q_x_loaded{s}") for s in range(GB)]
                stats_done, aggr_done, veps_done = sem("q_stats"), sem("q_aggr"), sem("q_veps")
                rstd_done, xn_done = sem("q_rstd"), sem("q_xn")
                t_done, xT_hi, xT_lo = sem("q_t_done"), sem("q_xT_hi"), sem("q_xT_lo")
                p_done, p_hi, p_lo = sem("q_p_done"), sem("q_p_hi"), sem("q_p_lo")
                NGRP, C = B // GB, NG * J
                assert C == 2 * GB

                def perm(a, g):
                    return a[:, :, g * J * P:(g + 1) * J * P].rearrange(
                        "p k (r j d) -> p k j r d", r=R, j=J)

                def wcols(a, k, g):
                    return a[:, k, g * J:(g + 1) * J, :].rearrange("p j (r d) -> p j r d", r=R)

                def xT_part(a, grp, n):
                    s, kh = n // 2, n % 2
                    return a[:, grp % 2, 4 * kh:4 * kh + 4, s * SQ:(s + 1) * SQ]

                def next_norm(grp, c):
                    t = GB * (grp + 1) + (c + 1) // 2
                    return t if c % 2 and t < B else None

                W_START = (), (), (0, 1), range(2, KT)

                with nc.Block() as block:
                    @block.sync
                    def _(sp):
                        wv_ = wq.rearrange("(k p) n -> p k n", p=P)

                        def load_x(t):
                            if t >= GB:
                                sp.wait_ge(t_done, 2 * (t - GB) + 2)
                            sp.dma_start(xn[:, t % GB, :], x[t]).then_inc(xin_loaded[t % GB], 16)

                        def load_w(g, k):
                            cols = slice(g * J * P, (g + 1) * J * P)
                            sp.dma_start(wraw[:, k, cols], wv_[:, k, cols]
                                         ).then_inc(w_loaded[KT if g else k], 16)
                        for s in range(GB - 1):
                            load_x(s)
                        load_w(0, 0)
                        load_x(GB - 1)
                        for k in range(1, KT):
                            load_w(0, k)
                        load_x(GB)
                        for k in range(KT):
                            load_w(1, k)
                        for t in range(GB + 1, 2 * GB):
                            load_x(t)
                        for n, w in enumerate((wk, wv)):
                            sp.dma_start(wkv_raw[:, :, n * KV:(n + 1) * KV],
                                         w.rearrange("(k p) n -> p k n", p=P)
                                         ).then_inc(wkv_loaded, 16)
                        for grp in range(NGRP):
                            for c in range(C):
                                sp.wait_ge(p_lo, C * grp + c + 1)
                                g, cols = c // J, slice(c % J * SQ, (c % J + 1) * SQ)
                                for hl, buf in enumerate((q_h, q_l)):
                                    sp.dma_start(
                                        q_scr[GB * grp:GB * (grp + 1), hl, :, g, cols].rearrange(
                                            "b p q -> p b q"),
                                        buf[:, c, :].bitcast(f32).rearrange("p (b q) -> p b q", q=SQ)
                                        ).then_inc(q_stored[c], 16)
                                t = GB * (grp + 2) + c // 2
                                if c % 2 and t < B:
                                    load_x(t)
                            if grp == 0:
                                sp.wait_ge(w_lo, KT * NG)
                                load_ctx(sp, 0, 0)
                                load_ctx(sp, 1, 1)
                    @block.gpsimd
                    def _(pool):
                        pool.memset(ident[:], 0.0).then_inc(consts, 1)
                        pool.memset(neghalf[:], -0.5).then_inc(consts, 1)
                        pool.wait_ge(consts, 2)
                        pool.affine_select(out=ident[:], in_=ident[:], compare_op=ALU.not_equal,
                                           fill=1.0, base=0, pattern=[[-1, P]],
                                           channel_multiplier=1).then_inc(consts, 1)
                        for t in range(B):
                            pool.wait_ge(veps_done, t + 1)
                            wait(pool, xn_done, t - 1)
                            pool.tensor_tensor(rstd[:, t % 2:t % 2 + 1], veps[:, t % 2:t % 2 + 1],
                                               neghalf[0:SQ, :], ALU.pow).then_inc(rstd_done, 1)

                    @block.vector
                    def _(dve):
                        def statistics(t):
                            slot = t % 2
                            dve.wait_ge(xin_loaded[t % GB], 16 * (t // GB + 1))
                            for h in range(2):
                                nc.vector.bn_stats(stats[:, h, :], xn[:, t % GB, h * FB:(h + 1) * FB]
                                                   ).then_inc(stats_done, 1)
                            dve.wait_ge(stats_done, 2 * t + 2)
                            wait(dve, xn_done, t - 1)
                            nc.vector.memset(hold[:, 2:3], 0.0)
                            nc.vector.bn_aggr(aggr[:, slot, :], stats[:]).then_inc(aggr_done, 1)
                            dve.wait_ge(aggr_done, t + 1)
                            nc.vector.tensor_scalar(veps[:, slot:slot + 1], aggr[:, slot, 1:2],
                                                    EPS, None, ALU.add).then_inc(veps_done, 1)

                        def normalise(t):
                            dve.wait_ge(rstd_done, t + 1)
                            nc.vector.tensor_scalar(xn[:, t % GB, :], xn[:, t % GB, :],
                                                    aggr[:, t % 2, 0:1], rstd[:, t % 2:t % 2 + 1],
                                                    ALU.subtract, ALU.mult).then_inc(xn_done, 1)

                        def split_w(g, k):
                            dve.wait_ge(w_hi, KT * g + k + 1)
                            to_lo(wcols(w_l, k, g), perm(wraw, g)[:, k], wcols(w_h, k, g)
                                  ).then_inc(w_lo, 1)

                        def split_x(grp, n):
                            dve.wait_ge(xT_hi, 2 * GB * grp + n + 1)
                            to_lo(xT_part(xT_l, grp, n),
                                  bank[n % 2][:, 0:4 * SQ].rearrange("p (k q) -> p k q", k=4),
                                  xT_part(xT_h, grp, n)).then_inc(xT_lo, 1)
                        def start(s):
                            for n in (2 * s, 2 * s + 1):
                                split_x(0, n)
                            for k in W_START[s]:
                                split_w(0, k)
                        statistics(0)
                        for s in range(GB):
                            if s + 1 < GB:
                                statistics(s + 1)
                            normalise(s)
                            if s:
                                start(s - 1)
                        start(GB - 1)
                        statistics(GB)
                        normalise(GB)
                        statistics(GB + 1)
                        for grp in range(NGRP):
                            for c in range(C):
                                if grp + 1 < NGRP:
                                    split_x(grp + 1, c)
                                dve.wait_ge(p_hi, C * grp + c + 1)
                                to_lo(q_l[:, c, :], bank[2 + c % 2][:, 0:GT], q_h[:, c, :]
                                      ).then_inc(p_lo, 1)
                                if grp == 0 and c < KT // 2:
                                    split_w(1, 2 * c)
                                    split_w(1, 2 * c + 1)
                                if next_norm(grp, c) is not None:
                                    normalise(next_norm(grp, c))
                                    if next_norm(grp, c) + 1 < B:
                                        statistics(next_norm(grp, c) + 1)

                    @block.scalar
                    def _(act):
                        def split_w(g, k):
                            if g == 0:
                                act.wait_ge(w_loaded[k], 16)
                            else:
                                act.wait_ge(w_loaded[KT], 16 * KT)
                            nc.scalar.activation(wcols(w_h, k, g), perm(wraw, g)[:, k], ACT.Copy
                                                 ).then_inc(w_hi, 1)

                        def split_x(grp, n):
                            if n == 0:
                                wait(act, p_done, C * (grp - 1))
                            act.wait_ge(t_done, 2 * GB * grp + n + 1)
                            nc.scalar.activation(
                                xT_part(xT_h, grp, n),
                                bank[n % 2][:, 0:4 * SQ].rearrange("p (k q) -> p k q", k=4),
                                ACT.Copy).then_inc(xT_hi, 1)
                        for s in range(GB):
                            for n in (2 * s, 2 * s + 1):
                                split_x(0, n)
                            for k in W_START[s]:
                                split_w(0, k)
                        for grp in range(NGRP):
                            for c in range(C):
                                if grp + 1 < NGRP:
                                    split_x(grp + 1, c)
                                act.wait_ge(p_done, C * grp + c + 1)
                                wait(act, q_stored[c], 32 * grp)
                                nc.scalar.activation(q_h[:, c, :], bank[2 + c % 2][:, 0:GT],
                                                     ACT.Copy).then_inc(p_hi, 1)
                                if grp == 0 and c < KT // 2:
                                    split_w(1, 2 * c)
                                    split_w(1, 2 * c + 1)

                    @block.tensor
                    def _(pe):
                        def transposes(grp, n):
                            s, kh = n // 2, n % 2
                            pe.wait_ge(xn_done, GB * grp + s + 1)
                            wait(pe, xT_lo, 2 * GB * grp + n - 1)
                            for k in range(4):
                                kk = 4 * kh + k
                                last = pe.transpose(bank[n % 2][:, k * SQ:(k + 1) * SQ],
                                                    xn[:, s, kk * P:(kk + 1) * P],
                                                    ident[0:SQ, 0:SQ])
                            last.then_inc(t_done, 1)
                        pe.wait_ge(consts, 3)
                        for n in range(2 * GB):
                            transposes(0, n)
                        for grp in range(NGRP):
                            pe.wait_ge(xT_lo, 2 * GB * (grp + 1))
                            for c in range(C):
                                wait(pe, p_lo, C * grp + c - 1)
                                for k in range(KT):
                                    if grp == 0 and c % J == 0:
                                        pe.wait_ge(w_lo, KT * (c // J) + k + 1)
                                    last = split_product(
                                        pe, bank[2 + c % 2][:, 0:GT],
                                        (w_h[:, k, c, :], w_l[:, k, c, :]),
                                        (xT_h[:, grp % 2, k, :], xT_l[:, grp % 2, k, :]),
                                        k == 0, k == KT - 1)
                                    if k == KT - 3 and grp + 1 < NGRP:
                                        transposes(grp + 1, c)
                                last.then_inc(p_done, 1)

        def attention():
            with ExitStack() as st:
                def sb(name, shape, dt=f32):
                    return st.enter_context(nc.sbuf_tensor("a_" + name, shape, dt))
                w_h, w_l = sb("w_h", [P, KT, 2 * KV], f32r), sb("w_l", [P, KT, 2 * KV], f32r)
                cT_h, cT_l = sb("cT_h", [P, 2, KT, SKP], f32r), sb("cT_l", [P, 2, KT, SKP], f32r)
                k_h, k_l = sb("k_h", [P, NG, SKP], f32r), sb("k_l", [P, NG, SKP], f32r)
                kst = sb("kst", [98, 2, NKV, SKP], f32r)
                qst = sb("qst", [98, 2, NKV, J * SQ], f32r)
                vnew = stash[0:CK, 2 * NC, 0:NC * KV].rearrange("p (c n) -> p c n", c=NC)
                v = stash[0:CK, 8:10, 0:NC * KV].rearrange("p s (c n) -> p s c n", c=NC)
                pr, prsum = sb("pr", [P, R, NC, J * SQ]), sb("prsum", [CK, R, J * SQ])
                o, l = sb("o", [P, NG, J * SQ]), sb("l", [P, NG, J * SQ])
                nm = sb("nm", [SQ, 2, NH])
                nm_h, nm_l = sb("nm_h", [NH, SQ], f32r), sb("nm_l", [NH, SQ], f32r)
                ones = sb("ones", [CK, HD])

                s_bank, st_bank, pj_bank = bank[0:2], bank[2:4], bank[4:6]
                o_bank, l_bank = bank[6], bank[7]
                w_hi, w_lo = sem("a_w_hi"), sem("a_w_lo")
                ready = sem("a_consts")
                t_done, t_hi, t_lo = sem("a_t_done"), sem("a_t_hi"), sem("a_t_lo")
                k_done, k_hi, k_lo = sem("a_k_done"), sem("a_k_hi"), sem("a_k_lo")
                v_done, v_out, v_moved = sem("a_v_done"), sem("a_v_out"), sem("a_v_moved")
                k_stored = sem("a_k_stored")
                kq_loaded = [[sem(f"a_kq_loaded{s}{g}") for g in range(NG)] for s in range(2)]
                s_done, max_done = sem("a_s_done"), sem("a_max_done")
                nmT_done, nm_hi, nm_lo = sem("a_nmT_done"), sem("a_nm_hi"), sem("a_nm_lo")
                nm_loaded = [sem("a_nm_loaded0"), sem("a_nm_loaded1")]
                st_done, exp_done, pv_done = sem("a_st_done"), sem("a_exp_done"), sem("a_pv_done")
                two_added, all_added = sem("a_two_added"), sem("a_all_added")
                sums_done, l_copied = sem("a_sums_done"), sem("a_l_copied")
                o_copied, l_inverted, o_scaled = sem("a_o_copied"), sem("a_l_inv"), sem("a_o_scaled")

                NT = 2 * NC
                NU = NG * NC * R

                STEPS, U0 = 32, 6
                KV_TILES = 3 * [[2, 1, 1, 1, 1, 2]] + [[2, 2, 1, 1, 2], [2, 2, 2, 1, 1]]
                T_STEP = {3: 0, 9: 1, 15: 2, 21: 3, 26: 4, 30: 5}
                KV_AT, KV_OUT = {}, {}
                at = 1
                for m, counts in enumerate(KV_TILES):
                    assert sum(counts) == KT
                    for n, count in enumerate(counts):
                        k = sum(counts[:n])
                        KV_AT[at] = m, range(k, k + count)
                        at += 1
                    KV_OUT[at] = m
                HEADS, h0 = [], 0
                for s in range(STEPS):
                    n = 0 if s >= STEPS - 2 else 2 if s in (18, 24) else 1
                    HEADS.append(range(h0, h0 + n))
                    h0 += n
                assert h0 == NH
                PV = {U0 + R * (NC * g + c + 1) + 1: (g, c) for g in range(NG) for c in range(NC)}
                SUMS = {2: (1, 1), 22: (0, 0)}
                INV = {25: (0, 0), 27: (0, 1), 28: (0, 2), 31: (0, 3),
                       5: (1, 0), 8: (1, 1), 11: (1, 2), 14: (1, 3)}

                def first(b):
                    return isinstance(b, int) and b == -3

                def kv_bank(par, m):
                    return pj_bank[(m + par) % 2]

                def t_bank(par, n):
                    return pj_bank[(n + (n < NT - 1) + par) % 2]

                def nm_bank(par):
                    return pj_bank[1 - par]

                def accumulated(eng, pb, m):
                    if m < NG:
                        eng.wait_ge(k_lo, NG * pb + m + 1)
                    else:
                        wait(eng, v_out, NC * pb + m - NG + 1)

                def cT_part(cT, par, n):
                    c, kh = n // 2, n % 2
                    return cT[:, 1 - par, 4 * kh:4 * kh + 4, c * CK:(c + 1) * CK]

                def w_tiles(b, n):
                    return () if not first(b) else (n,) if n < NT - 1 else range(n, KT)

                def each(eng, body):
                    body(-2, 1, True, False, False, False)
                    body(-1, 0, True, True, False, False)
                    body(-1, 1, True, True, True, False)
                    body(0, 0, True, True, True, True)
                    body(0, 1, True, True, True, True)
                    with eng.Fori(1, B // 2 - 2) as i:
                        body(i, 0, True, True, True, True)
                        body(i, 1, True, True, True, True)
                    body(B // 2 - 2, 0, True, True, True, True)
                    body(B // 2 - 2, 1, False, True, True, True)
                    body(B // 2 - 1, 0, False, False, True, True)
                    body(B // 2 - 1, 1, False, False, False, True)

                with nc.Block() as block:
                    @block.sync
                    def _(sp):
                        def store(b, g):
                            sp.wait_ge(o_scaled, NG * b + g + 1)
                            sp.dma_start(a_scr[:, g * J:(g + 1) * J, bass.ds(b * SQ, SQ)],
                                         o[:, g, :].rearrange("p (j q) -> p j q", j=J)
                                         ).then_inc(o_stored[g], 16)

                        def body(i, par, trans, proj, score, attn):
                            b = 2 * i + par
                            pb = b + 2
                            if attn:
                                sp.wait_ge(nm_lo, b + 1)
                                for row, src in ((96, nm_h), (97, nm_l)):
                                    sp.dma_start(qst[row:row + 1, par, :, :].bitcast(f32).rearrange(
                                        "o g (j q) -> o (g j) q", j=J), src[:, :].bitcast(f32)
                                        ).then_inc(nm_loaded[par], 16)
                            if attn and not (isinstance(b, int) and b == 0):
                                store(b - 1, 0)
                            if not isinstance(b, int) or -2 <= b < B - 4:
                                sp.wait_ge(t_done, NT * (b + 3))
                                load_ctx(sp, b + 4, par)
                            if isinstance(b, int) and b == B - 2:
                                sp.wait_ge(t_done, NT * B)
                                sp.wait_ge(v_moved, B)
                                load_wo(sp, 0, range(KT))
                            if isinstance(b, int) and b == -2:
                                for stored in q_stored:
                                    sp.wait_ge(stored, 32 * (B // GB))
                            if proj:
                                sp.wait_ge(k_lo, NG * (pb + 1))
                                for hl, buf in enumerate((k_h, k_l)):
                                    sp.dma_start(k_scr[par, hl].rearrange("g p n -> p g n"),
                                                 buf[:, :, :].bitcast(f32)).then_inc(k_stored, 16)
                                sp.wait_ge(k_stored, 32 * (pb + 1))
                                load_stacks(i, par, b, 0)
                            if attn and not (isinstance(b, int) and b == 0):
                                store(b - 1, 1)
                            if proj:
                                load_stacks(i, par, b, 1)

                        def load_stacks(i, par, b, g):
                            pb = b + 2
                            wait(sp, st_done, NU * b + NC * R * (g + 1))
                            heads = slice(g * R, (g + 1) * R)
                            for m, (khl, qhl) in enumerate(((0, 0), (1, 0), (0, 1))):
                                rows = slice(m * HD, (m + 1) * HD)
                                sp.dma_start(kst[rows, par, heads, :].bitcast(f32),
                                             k_scr[par, khl, g].rearrange("(r d) n -> d r n", r=R)
                                             ).then_inc(kq_loaded[par][g], 16)
                                sp.dma_start(qst[rows, par, heads, :].bitcast(f32),
                                             q_scr[bass.ds(pb, 1), qhl, :, g].rearrange(
                                                 "b (r d) n -> d (b r) n", r=R)
                                             ).then_inc(kq_loaded[par][g], 16)

                        each(sp, body)
                        sp.wait_ge(pv_done, NC * NG * (B - 1))
                        load_tile(sp, 0, 0, 0)
                        store(B - 1, 0)
                        store(B - 1, 1)

                    @block.gpsimd
                    def _(pool):
                        pool.memset(ones[:], 1.0).then_inc(ready, 1)
                        pool.wait_ge(ready, 1)
                        pool.memset(kst[96:98, :, :, :].bitcast(f32).rearrange("p s g n -> p (s g n)"), 1.0
                                    ).then_inc(ready, 1)
                        pool.wait_ge(ready, 2)
                        for cT in (cT_h, cT_l):
                            pool.memset(cT[:, :, :, SK:SKP].bitcast(f32), 0.0).then_inc(ready, 1)

                        def add(b, g, last):
                            n = NG * b + g
                            pool.wait_ge(exp_done, R * (NC * n + 2 + last))
                            if last:
                                pool.wait_ge(two_added, n + 1)
                                pool.tensor_tensor(prsum[:], prsum[:], pr[0:CK, :, 2, :], ALU.add
                                                   ).then_inc(all_added, 1)
                            else:
                                wait(pool, sums_done, n)
                                pool.tensor_tensor(prsum[:], pr[0:CK, :, 0, :], pr[0:CK, :, 1, :],
                                                   ALU.add).then_inc(two_added, 1)

                        def scale(b, g):
                            n = NG * b + g
                            pool.wait_ge(o_copied, n + 1)
                            pool.wait_ge(l_inverted, J * (n + 1))
                            pool.tensor_tensor(o[:, g, :], o[:, g, :], l[:, g, :], ALU.mult
                                               ).then_inc(o_scaled, 1)

                        def body(i, par, trans, proj, score, attn):
                            b = 2 * i + par
                            if attn:
                                add(b, 0, 0)
                                if not (isinstance(b, int) and b == 0):
                                    scale(b - 1, 1)
                                add(b, 0, 1)
                                add(b, 1, 0)
                                add(b, 1, 1)
                                scale(b, 0)
                        each(pool, body)
                        scale(B - 1, 1)

                    @block.vector
                    def _(dve):
                        def invert(b, g, j):
                            dve.wait_ge(l_copied, NG * b + g + 1)
                            part = l[:, g, j * SQ:(j + 1) * SQ]
                            nc.vector.reciprocal(part, part).then_inc(l_inverted, 1)

                        def body(i, par, trans, proj, score, attn):
                            b = 2 * i + par
                            sb_, pb, tb = b + 1, b + 2, b + 3
                            for s in range(STEPS):
                                if attn and s == 0:
                                    dve.wait_ge(nmT_done, b + 1)
                                    wait(dve, nm_loaded[1 - par], 32 * (i + par))
                                    nc.vector.tensor_copy(nm_h[:], nm_bank(par)[0:NH, 0:SQ]
                                                          ).then_inc(nm_hi, 1)
                                    dve.wait_ge(nm_hi, b + 1)
                                    to_lo(nm_l[:], nm_bank(par)[0:NH, 0:SQ], nm_h[:]
                                          ).then_inc(nm_lo, 1)
                                if score:
                                    for h in HEADS[s]:
                                        dve.wait_ge(s_done, NH * sb_ + h + 1)
                                        nc.vector.tensor_reduce(nm[:, 1 - par, h:h + 1],
                                                                s_bank[h % 2][0:SQ, 0:SK], AX.X,
                                                                ALU.max, negate=True
                                                                ).then_inc(max_done, 1)
                                if proj and s in KV_OUT:
                                    m = KV_OUT[s]
                                    if m < NG:
                                        dve.wait_ge(k_hi, NG * pb + m + 1)
                                        to_lo(k_l[:, m, :], kv_bank(par, m)[:, 0:SKP], k_h[:, m, :]
                                              ).then_inc(k_lo, 1)
                                    else:
                                        c = m - NG
                                        dve.wait_ge(v_done, NC * pb + c + 1)
                                        if c == 0:
                                            wait(dve, v_moved, pb)
                                        nc.vector.tensor_copy(vnew[:, c, :],
                                                              kv_bank(par, m)[0:CK, 0:KV]
                                                              ).then_inc(v_out, 1)
                                if trans and s in T_STEP:
                                    n = T_STEP[s]
                                    dve.wait_ge(t_hi, NT * tb + n + 1)
                                    to_lo(cT_part(cT_l, par, n), t_bank(par, n)[:, 0:4 * CK].rearrange(
                                        "p (k n) -> p k n", k=4), cT_part(cT_h, par, n)
                                        ).then_inc(t_lo, 1)
                                    for k in w_tiles(b, n):
                                        dve.wait_ge(w_hi, k + 1)
                                        to_lo(w_l[:, k, :], wkv_raw[:, k, :], w_h[:, k, :]
                                              ).then_inc(w_lo, 1)
                                if score and s == 10:
                                    dve.wait_ge(v_out, NC * (sb_ + 1))
                                    wait(dve, pv_done, NC * NG * b)
                                    nc.vector.tensor_copy(v[:, 1 - par, :, :], vnew[:, :, :]
                                                          ).then_inc(v_moved, 1)
                                if attn and s in INV:
                                    g, j = INV[s]
                                    if g == 0:
                                        invert(b, 0, j)
                                    elif not (isinstance(b, int) and b == 0):
                                        invert(b - 1, 1, j)
                        each(dve, body)
                        for j in range(J):
                            invert(B - 1, 1, j)

                    @block.scalar
                    def _(act):
                        act.wait_ge(wkv_loaded, 32)

                        def copy_out(b, g):
                            act.wait_ge(pv_done, NC * (NG * b + g + 1))
                            wait(act, o_stored[g], 16 * b)
                            nc.scalar.activation(o[:, g, :], o_bank[:, 0:J * SQ], ACT.Copy
                                                 ).then_inc(o_copied, 1)

                        def copy_sums(b, g):
                            act.wait_ge(sums_done, NG * b + g + 1)
                            wait(act, o_scaled, NG * (b - 1) + g + 1)
                            nc.scalar.activation(l[:, g, :], l_bank[:, 0:J * SQ], ACT.Copy
                                                 ).then_inc(l_copied, 1)

                        def body(i, par, trans, proj, score, attn):
                            b = 2 * i + par
                            pb, tb = b + 2, b + 3
                            for s in range(STEPS):
                                if proj and s in KV_OUT and KV_OUT[s] < NG:
                                    g = KV_OUT[s]
                                    act.wait_ge(k_done, NG * pb + g + 1)
                                    if g == 0:
                                        wait(act, k_stored, 32 * pb)
                                    nc.scalar.activation(k_h[:, g, :], kv_bank(par, g)[:, 0:SKP], ACT.Copy
                                                         ).then_inc(k_hi, 1)
                                if trans and s in T_STEP:
                                    n = T_STEP[s]
                                    act.wait_ge(t_done, NT * tb + n + 1)
                                    if n == 0:
                                        wait(act, v_done, NC * pb)
                                    nc.scalar.activation(cT_part(cT_h, par, n),
                                                         t_bank(par, n)[:, 0:4 * CK].rearrange(
                                                             "p (k n) -> p k n", k=4), ACT.Copy
                                                         ).then_inc(t_hi, 1)
                                    for k in w_tiles(b, n):
                                        nc.scalar.activation(w_h[:, k, :], wkv_raw[:, k, :], ACT.Copy
                                                             ).then_inc(w_hi, 1)
                                if attn and s == 1 and not (isinstance(b, int) and b == 0):
                                    copy_out(b - 1, 1)
                                if attn and s - 1 in SUMS:
                                    g, back = SUMS[s - 1]
                                    if not (isinstance(b, int) and b < back):
                                        copy_sums(b - back, g)
                                if attn and 0 <= s - U0 < NU:
                                    u = s - U0
                                    g, c, r = u // (NC * R), u // R % NC, u % R
                                    act.wait_ge(st_done, NU * b + u + 1)
                                    if isinstance(b, int) and b == 0 and u == 0:
                                        for stored in q_stored:
                                            act.wait_ge(stored, 32 * (B // GB))
                                    if r == 0:
                                        wait(act, pv_done, NC * (NG * b + g - 1) + c + 1)
                                        if c != 1:
                                            wait(act, all_added if c == 2 else two_added, NG * b + g)
                                    nc.scalar.activation(pr[0:CK, r, c, :],
                                                         st_bank[u % 2][0:CK, 0:J * SQ], ACT.Exp,
                                                         scale=SCALE).then_inc(exp_done, 1)
                                if attn and s == 20:
                                    copy_out(b, 0)
                        each(act, body)
                        copy_out(B - 1, 1)
                        copy_sums(B - 1, 1)

                    @block.tensor
                    def _(pe):
                        def sums(b, g):
                            pe.wait_ge(all_added, NG * b + g + 1)
                            wait(pe, l_copied, NG * b + g)
                            for r in range(R):
                                last = pe.matmul(l_bank[r * HD:(r + 1) * HD, 0:J * SQ], ones[:, :],
                                                 prsum[:, r, :], start=True, stop=True)
                            last.then_inc(sums_done, 1)

                        def body(i, par, trans, proj, score, attn):
                            b = 2 * i + par
                            sb_, pb, tb = b + 1, b + 2, b + 3
                            for s in range(STEPS):
                                for h in HEADS[s] if score else ():
                                    g, j = h // J, h % J
                                    if h % (NH // NG) == 0:
                                        pe.wait_ge(kq_loaded[1 - par][h * NG // NH],
                                                   96 * (i + par + 1))
                                    wait(pe, max_done, NH * sb_ + h - 1)
                                    pe.matmul(s_bank[h % 2][0:SQ, 0:SKP],
                                              qst[0:96, 1 - par, g, j * SQ:(j + 1) * SQ],
                                              kst[0:96, 1 - par, g, :], start=True, stop=True
                                              ).then_inc(s_done, 1)
                                if attn and s == 0:
                                    pe.wait_ge(max_done, NH * (b + 1))
                                    done = NC * (b + 2)
                                    pe.wait_ge(v_out, min(done, NC * B) if isinstance(done, int)
                                               else done)
                                    pe.transpose(nm_bank(par)[0:NH, 0:SQ], nm[:, par, :],
                                                 ident[0:SQ, 0:SQ]).then_inc(nmT_done, 1)
                                if trans and s in T_STEP:
                                    n = T_STEP[s]
                                    c, kh = n // 2, n % 2
                                    if n == 0:
                                        pe.wait_ge(c_loaded[1 - par], 16 * NC * (i + 2 + par))
                                    if n == NT - 1:
                                        pe.wait_ge(t_lo, NT * tb + n)
                                    elif n == 0 and attn:
                                        pe.wait_ge(nm_lo, b + 1)
                                    elif proj:
                                        accumulated(pe, pb, n - 1)
                                    else:
                                        wait(pe, t_lo, n - 1)
                                    for k in range(4):
                                        kk = 4 * kh + k
                                        last = pe.transpose(t_bank(par, n)[:, k * CK:(k + 1) * CK],
                                                            ctx_in[:, 1 - par, c, kk * P:(kk + 1) * P],
                                                            ident[0:CK, 0:CK])
                                    last.then_inc(t_done, 1)
                                if proj and s in KV_AT:
                                    m, ks = KV_AT[s]
                                    if m == 0 and ks[0] == 0:
                                        if isinstance(b, int) and b == -2:
                                            pe.wait_ge(w_lo, KT)
                                            pe.wait_ge(ready, 4)
                                        pe.wait_ge(t_lo, NT * (pb + 1))
                                    elif ks[0] == 0:
                                        if trans:
                                            pe.wait_ge(t_lo, NT * tb + m)
                                        elif m == 1:
                                            pe.wait_ge(nm_lo, b + 1)
                                        else:
                                            accumulated(pe, pb, m - 2)
                                    for k in ks:
                                        if m < NG:
                                            part = slice(m * P, (m + 1) * P)
                                            last = split_product(
                                                pe, kv_bank(par, m)[:, 0:SKP],
                                                (w_h[:, k, part], w_l[:, k, part]),
                                                (cT_h[:, par, k, :], cT_l[:, par, k, :]),
                                                k == 0, k == KT - 1)
                                        else:
                                            keys = slice((m - NG) * CK, (m - NG + 1) * CK)
                                            last = split_product(
                                                pe, kv_bank(par, m)[0:CK, 0:KV],
                                                (cT_h[:, par, k, keys], cT_l[:, par, k, keys]),
                                                (w_h[:, k, KV:2 * KV], w_l[:, k, KV:2 * KV]),
                                                k == 0, k == KT - 1)
                                    if ks[-1] == KT - 1:
                                        last.then_inc(k_done if m < NG else v_done, 1)
                                if attn and 0 <= s - U0 < NU:
                                    u = s - U0
                                    g, c, r = u // (NC * R), u // R % NC, u % R
                                    if u == 0:
                                        pe.wait_ge(nm_loaded[par], 32 * (i + 1))
                                    wait(pe, exp_done, NU * b + u - 1)
                                    pe.matmul(st_bank[u % 2][0:CK, 0:J * SQ],
                                              kst[0:98, par, g * R + r, c * CK:(c + 1) * CK],
                                              qst[0:98, par, g * R + r, :], start=True, stop=True
                                              ).then_inc(st_done, 1)
                                if attn and s in SUMS:
                                    g, back = SUMS[s]
                                    if not (isinstance(b, int) and b < back):
                                        sums(b - back, g)
                                if attn and s in PV:
                                    g, c = PV[s]
                                    if c == 0:
                                        wait(pe, o_copied, NG * b + g)
                                        pe.wait_ge(v_moved, b + 1)
                                    pe.wait_ge(exp_done, NU * b + R * (NC * g + c + 1))
                                    for r in range(R):
                                        h = (g * R + r) * HD
                                        last = pe.matmul(
                                            o_bank[r * HD:(r + 1) * HD, 0:J * SQ],
                                            v[:, par, c, h:h + HD], pr[0:CK, r, c, :],
                                            start=c == 0, stop=c == NC - 1)
                                    last.then_inc(pv_done, 1)
                        each(pe, body)
                        sums(B - 1, 1)

        def mixing(half, y, x2_h, x2_l):
            with ExitStack() as st:
                C = NG * J

                def sb(name, shape, dt=f32):
                    return st.enter_context(nc.sbuf_tensor(f"m{half}_{name}", shape, dt))

                def s_(name):
                    return sem(f"m{half}_{name}")
                w_h, w_l = sb("w_h", [P, C, D], f32r), sb("w_l", [P, C, D], f32r)
                a_h, a_l = sb("a_h", [P, 2, C, P], f32r), sb("a_l", [P, 2, C, P], f32r)
                xn = sb("xn", [P, 2, D])
                stats, aggr = sb("stats", [P, 2, 6]), sb("aggr", [P, 2])
                veps, rstd = sb("veps", [P, 1]), sb("rstd", [P, 1])
                w_hi, w_lo = s_("w_hi"), s_("w_lo")
                a_hi, a_lo = s_("a_hi"), s_("a_lo")
                o_done, y_done = s_("o_done"), s_("y_done")
                stats_done, aggr_done, veps_done = s_("stats"), s_("aggr"), s_("veps")
                rstd_done, xn_done = s_("rstd"), s_("xn")
                t_done, t_hi, t_lo = s_("t_done"), s_("t_hi"), s_("t_lo")
                o_bank, t_bank = bank[0:2], bank[2:4]

                def tiles(eng, step):
                    step(1, 1, 0)
                    with eng.Fori(1, TT // 2) as i:
                        step(2 * i, 0, i)
                        step(2 * i + 1, 1, i)
                    step(TT - 1, 0, TT // 2)

                with nc.Block() as block:
                    @block.sync
                    def _(sp):
                        if half == 0:
                            for stored in o_stored:
                                sp.wait_ge(stored, 16 * B)
                            load_tile(sp, 0, 1, 1)
                        sp.wait_ge(w_lo, C)
                        if half == 0:
                            load_scales(sp)
                        for par in range(2):
                            load13(sp, half, 0, par)
                        for par in range(2):
                            load2(sp, half, 0, par)
                        with sp.Fori(0, TT // 2 - 1) as i:
                            for t, slot in ((2 * i + 2, 0), (2 * i + 3, 1)):
                                sp.wait_ge(y_done, 2 * (t - 1))
                                load_tile(sp, half, t, slot)
                        sp.wait_ge(y_done, 2 * (TT - 2))
                        load_tile(sp, half, TT - 1, 0)

                    @block.gpsimd
                    def _(pool):
                        def inverse_deviations(first, last):
                            with pool.Fori(first, last) as t:
                                pool.wait_ge(veps_done, t + 1)
                                pool.tensor_tensor(rstd[:], veps[:], neghalf[:], ALU.pow
                                                   ).then_inc(rstd_done, 1)
                        inverse_deviations(0, TT // 2)
                        if half == 0:
                            pool.wait_ge(sc_loaded, 48)
                            for par in range(2):
                                scale13(pool, 0, par)
                        inverse_deviations(TT // 2, TT)

                    @block.scalar
                    def _(act):
                        def split_attention(t, slot, use):
                            act.wait_ge(a_loaded[half][slot], 16 * (use + 1))
                            wait(act, o_done, 2 * (t - 1))
                            nc.scalar.activation(a_h[:, slot, :, :], attn_in[:, slot, :, :], ACT.Copy
                                                 ).then_inc(a_hi, 1)

                        def split_x(t):
                            for kh in range(2):
                                act.wait_ge(t_done, 2 * t + kh + 1)
                                nc.scalar.activation(
                                    x2_h[:, 4 * kh:4 * kh + 4, bass.ds(t * P, P)],
                                    t_bank[kh][:, :].rearrange("p (k q) -> p k q", k=4), ACT.Copy
                                ).then_inc(t_hi, 1)
                        split_attention(0, 0, 0)
                        act.wait_ge(wo_loaded[half], 16 * R * C)
                        for c in range(C):
                            nc.scalar.activation(w_h[:, c, :], wo_raw[:, c, :], ACT.Copy
                                                 ).then_inc(w_hi, 1)
                        split_attention(1, 1, 0)

                        def step(t, slot, use):
                            if not (isinstance(t, int) and t == TT - 1):
                                split_attention(t + 1, 1 - slot, use + slot)
                            split_x(t - 1)
                        tiles(act, step)
                        split_x(TT - 1)

                    @block.vector
                    def _(dve):
                        def split_attention(t, slot):
                            dve.wait_ge(a_hi, t + 1)
                            to_lo(a_l[:, slot, :, :], attn_in[:, slot, :, :], a_h[:, slot, :, :]
                                  ).then_inc(a_lo, 1)

                        def residual_norm(t, slot, use):
                            dve.wait_ge(x_loaded[half][slot], 16 * (use + 1))
                            for n in range(2):
                                cols = slice(n * FB, (n + 1) * FB)
                                dve.wait_ge(o_done, 2 * t + n + 1)
                                nc.vector.tensor_tensor(y[:, bass.ds(t, 1), cols].rearrange(
                                    "p t n -> p (t n)"), o_bank[n][:, :],
                                    x_in[:, slot, cols], ALU.add).then_inc(y_done, 1)
                                dve.wait_ge(y_done, 2 * t + n + 1)
                                nc.vector.memset(hold[:, n:n + 1], 0.0)
                                nc.vector.bn_stats(stats[:, n, :], y[:, bass.ds(t, 1), cols].rearrange(
                                    "p t n -> p (t n)")).then_inc(stats_done, 1)
                            dve.wait_ge(stats_done, 2 * t + 2)
                            nc.vector.memset(hold[:, 2:3], 0.0)
                            nc.vector.bn_aggr(aggr[:], stats[:]).then_inc(aggr_done, 1)
                            dve.wait_ge(aggr_done, t + 1)
                            nc.vector.tensor_scalar(veps[:], aggr[:, 1:2], EPS, None, ALU.add
                                                    ).then_inc(veps_done, 1)
                            dve.wait_ge(rstd_done, t + 1)
                            wait(dve, t_done, 2 * (t - 1))
                            nc.vector.tensor_scalar(xn[:, slot, :], y[:, bass.ds(t, 1), :].rearrange(
                                "p t n -> p (t n)"), aggr[:, 0:1], rstd[:], ALU.subtract, ALU.mult
                                ).then_inc(xn_done, 1)

                        def split_x(t):
                            for kh in range(2):
                                dst = (slice(None), slice(4 * kh, 4 * kh + 4), bass.ds(t * P, P))
                                dve.wait_ge(t_hi, 2 * t + kh + 1)
                                to_lo(x2_l[dst], t_bank[kh][:, :].rearrange(
                                    "p (k q) -> p k q", k=4), x2_h[dst]).then_inc(t_lo, 1)
                        split_attention(0, 0)
                        for c in range(C):
                            dve.wait_ge(w_hi, c + 1)
                            to_lo(w_l[:, c, :], wo_raw[:, c, :], w_h[:, c, :]).then_inc(w_lo, 1)
                        split_attention(1, 1)
                        if half:
                            dve.wait_ge(y_stored[0], 16 * TT)
                        else:
                            for stored in o_stored:
                                dve.wait_ge(stored, 16 * B)
                        residual_norm(0, 0, 0)

                        def step(t, slot, use):
                            if not (isinstance(t, int) and t == TT - 1):
                                split_attention(t + 1, 1 - slot)
                            residual_norm(t, slot, use)
                            split_x(t - 1)
                        tiles(dve, step)
                        split_x(TT - 1)

                    @block.tensor
                    def _(pe):
                        def product(slot, n, c):
                            cols = slice(n * FB, (n + 1) * FB)
                            return split_product(
                                pe, o_bank[n][:, :], (a_h[:, slot, c, :], a_l[:, slot, c, :]),
                                (w_h[:, c, cols], w_l[:, c, cols]), c == 0, c == C - 1)

                        def products(t, slot):
                            pe.wait_ge(a_lo, t + 1)
                            for n in range(2):
                                pe.wait_ge(y_done, 2 * t + n - 1)
                                for c in range(C):
                                    last = product(slot, n, c)
                                last.then_inc(o_done, 1)

                        def transposes(t, slot):
                            pe.wait_ge(xn_done, t + 1)
                            for kh in range(2):
                                wait(pe, t_lo, 2 * t + kh - 1)
                                for k in range(4):
                                    kk = 4 * kh + k
                                    last = pe.transpose(t_bank[kh][:, k * P:(k + 1) * P],
                                                        xn[:, slot, kk * P:(kk + 1) * P], ident[:])
                                last.then_inc(t_done, 1)
                        pe.wait_ge(a_lo, 1)
                        for c in range(C):
                            pe.wait_ge(w_lo, c + 1)
                            for n in range(2):
                                last = product(0, n, c)
                                if c == C - 1:
                                    last.then_inc(o_done, 1)

                        def step(t, slot, use):
                            products(t, slot)
                            transposes(t - 1, 1 - slot)
                        tiles(pe, step)
                        transposes(TT - 1, 0)

        def ffn(half, y, x2_h, x2_l):
            with ExitStack() as st:
                def sb(name, shape, dt=f32):
                    return st.enter_context(nc.sbuf_tensor(f"f{half}_{name}", shape, dt))

                def s_(name):
                    return sem(f"f{half}_{name}")
                w13_h = sb("w13_h", [P, 2, 2, KT, P], f32r)
                w13_l = sb("w13_l", [P, 2, 2, KT, P], f32r)
                w2_h, w2_l = sb("w2_h", [P, 2, D], f32r), sb("w2_l", [P, 2, D], f32r)
                if half == 0:
                    wt = sb("wt", [P, 3, D])
                gate, hf = sb("gate", [P, 2, TB]), sb("hf", [P, 2, TB])
                h_h, h_l = sb("h_h", [P, 2, HALF], f32r), sb("h_l", [P, 2, HALF], f32r)
                g_bank, u_bank, y_bank, t_bank = bank[0:2], bank[2:4], bank[4:6], bank[6:8]
                scaled2 = s_("scaled2")
                t13_done, t2_done = s_("t13_done"), s_("t2_done")
                t_hi, t_lo = s_("t_hi"), s_("t_lo")
                g_done, u_done, silu_done = s_("g_done"), s_("u_done"), s_("silu")
                h_done, h_hi, h_lo = s_("h_done"), s_("h_hi"), s_("h_lo")
                y_done, y_added = s_("y_done"), s_("y_added")
                NP = NI // 2
                NY = 2 * TT
                T13, T2 = 4, 2
                PER = 2 * (T13 + T2)

                def t13_first(p, par):
                    return PER * p + T13 * par

                def t2_first(p, par):
                    return PER * p + 2 * T13 + T2 * par

                with nc.Block() as block:
                    @block.sync
                    def _(sp):
                        if half == 0:
                            for t in range(2):
                                load_tile(sp, 1, t, t)
                        def store_wt(first_bank, slot, chunk, m):
                            sp.wait_ge(t_hi, first_bank + 2)
                            sp.dma_start(wt_scr[bass.ds(chunk, 1), m].rearrange("a p n -> (a p) n"),
                                         wt[:, slot, :]).then_inc(wt_stored[slot], 16)

                        def store_wt13(p, par):
                            for m in range(2):
                                store_wt(t13_first(p, par) + 2 * m, (2 * par + m) % 3,
                                         2 * p + par, m)

                        def store_wt2(p, par):
                            store_wt(t2_first(p, par), (4 + par) % 3, 2 * p + par, 2)

                        if half == 0:
                            for par in range(2):
                                store_wt13(0, par)
                            with sp.Fori(0, NP - 1) as p:
                                for par in range(2):
                                    sp.wait_ge(t13_done, T13 * (2 * p + par + 1))
                                    load13(sp, half, p + 1, par)
                                for par in range(2):
                                    sp.wait_ge(t2_done, T2 * (2 * p + par + 1))
                                    load2(sp, half, p + 1, par)
                                    store_wt2(p, par)
                                for par in range(2):
                                    store_wt13(p + 1, par)
                            load_wo(sp, 1, range(4))
                            for par in range(2):
                                store_wt2(NP - 1, par)
                            load_wo(sp, 1, range(4, KT))
                        else:
                            with sp.Fori(0, NP - 1) as p:
                                for par in range(2):
                                    sp.wait_ge(t_lo, t13_first(p, par) + T13)
                                    load13(sp, half, p + 1, par)
                                for par in range(2):
                                    sp.wait_ge(t_lo, t2_first(p, par) + T2)
                                    load2(sp, half, p + 1, par)
                        of = out.rearrange("b q n -> (b q) n")
                        for t in range(TT):
                            sp.wait_ge(y_added, NY * (NP - 1) + 2 * (t + 1))
                            tok = half * HALF + t * P
                            sp.dma_start(of[tok:tok + P, :], y[:, t, :]).then_inc(y_stored[half], 16)
                        if half == 0:
                            for stored in wt_stored:
                                sp.wait_ge(stored, 16 * NI)
                        else:
                            for h in range(2):
                                sp.wait_ge(y_stored[h], 16 * TT)

                    @block.gpsimd
                    def _(pool):
                        def scale2(p, par):
                            pool.wait_ge(r2_loaded[0][par], 16 * (p + 1))
                            w = raw2[:, par, :, :]
                            s = sc2[:, :, bass.ds(2 * p + par, 1)].broadcast_to([P, KT, P])
                            pool.tensor_tensor(w, w, s, ALU.mult).then_inc(scaled2, 1)
                        if half == 0:
                            for par in range(2):
                                scale2(0, par)
                            with pool.Fori(1, NP) as p:
                                for par in range(2):
                                    scale13(pool, p, par)
                                for par in range(2):
                                    scale2(p, par)

                    def transposed13(par, n):
                        m, kh = n // 2, n % 2
                        return tuple(w[:, par, m, 4 * kh:4 * kh + 4, :].rearrange("p k i -> p (k i)")
                                     for w in (w13_h, w13_l))

                    def transposed2(par, n):
                        return tuple(w[:, par, n * FB:(n + 1) * FB] for w in (w2_h, w2_l))

                    def source13(par, n):
                        return t_bank[n % 2][:, :] if half == 0 else raw13[
                            :, par, n // 2, n % 2 * FB:(n % 2 + 1) * FB]

                    def source2(par, n):
                        return t_bank[n % 2][:, :] if half == 0 else raw2[
                            :, par, 4 * n:4 * n + 4, :].rearrange("p n i -> p (n i)")

                    @block.scalar
                    def _(act):
                        def copy_bank(n, slot, reused):
                            if n % 2 == 0:
                                wait(act, wt_stored[slot], 16 * reused)
                            nc.scalar.activation(wt[:, slot, n % 2 * FB:(n % 2 + 1) * FB],
                                                 t_bank[n % 2][:, :], ACT.Copy)

                        def split13(p, par):
                            if half == 1:
                                act.wait_ge(r13_loaded[1][par], 32 * (p + 1))
                                wait(act, u_done, 4 * (p - 1) + 2 * par + 2)
                            for n in range(T13):
                                if half == 0:
                                    act.wait_ge(t13_done, T13 * (2 * p + par) + n + 1)
                                    unit = 2 * par + n // 2
                                    copy_bank(n, unit % 3, 2 * p + unit // 3)
                                nc.scalar.activation(transposed13(par, n)[0], source13(par, n),
                                                     ACT.Copy).then_inc(t_hi, 1)

                        def split2(p, par):
                            if half == 1:
                                act.wait_ge(r2_loaded[1][par], 16 * (p + 1))
                                wait(act, y_done, NY * p)
                            for n in range(T2):
                                if half == 0:
                                    act.wait_ge(t2_done, T2 * (2 * p + par) + n + 1)
                                    unit = 4 + par
                                    copy_bank(n, unit % 3, 2 * p + unit // 3)
                                nc.scalar.activation(transposed2(par, n)[0], source2(par, n),
                                                     ACT.Copy).then_inc(t_hi, 1)

                        def gates(p, par, tb):
                            n = 4 * p + 2 * par + tb
                            act.wait_ge(g_done, n + 1)
                            wait(act, h_done, n - 1)
                            nc.scalar.activation(gate[:, tb, :], g_bank[tb][:, 0:TB], ACT.Silu
                                                 ).then_inc(silu_done, 1)
                            act.wait_ge(h_done, n + 1)
                            wait(act, y_done, NY * p)
                            nc.scalar.activation(h_h[:, par, tb * TB:(tb + 1) * TB], hf[:, tb, :],
                                                 ACT.Copy).then_inc(h_hi, 1)
                        split13(0, 0)
                        split13(0, 1)

                        def pair(p, more):
                            if isinstance(p, int) and p == 0:
                                gates(p, 0, 0)
                            split2(p, 0)
                            split2(p, 1)
                            if not (isinstance(p, int) and p == 0):
                                gates(p, 0, 0)
                            gates(p, 0, 1)
                            if more:
                                split13(p + 1, 0)
                            gates(p, 1, 0)
                            gates(p, 1, 1)
                            if more:
                                split13(p + 1, 1)
                        pair(0, True)
                        with act.Fori(1, NP - 1) as p:
                            pair(p, True)
                        pair(NP - 1, False)

                    @block.vector
                    def _(dve):
                        def split13(p, par, banks=range(T13)):
                            for n in banks:
                                hi, lo = transposed13(par, n)
                                dve.wait_ge(t_hi, t13_first(p, par) + n + 1)
                                to_lo(lo, source13(par, n), hi).then_inc(t_lo, 1)

                        def split2(p, par):
                            for n in range(T2):
                                hi, lo = transposed2(par, n)
                                dve.wait_ge(t_hi, t2_first(p, par) + n + 1)
                                to_lo(lo, source2(par, n), hi).then_inc(t_lo, 1)

                        def hidden(p, par, tb):
                            n = 4 * p + 2 * par + tb
                            dve.wait_ge(silu_done, n + 1)
                            dve.wait_ge(u_done, n + 1)
                            wait(dve, h_lo, n - 1)
                            nc.vector.tensor_tensor(hf[:, tb, :], u_bank[tb][:, 0:TB],
                                                    gate[:, tb, :], ALU.mult).then_inc(h_done, 1)
                            dve.wait_ge(h_hi, n + 1)
                            cols = slice(tb * TB, (tb + 1) * TB)
                            to_lo(h_l[:, par, cols], hf[:, tb, :], h_h[:, par, cols]
                                  ).then_inc(h_lo, 1)

                        def add_y(p, tiles):
                            for t in tiles:
                                for n in range(2):
                                    dve.wait_ge(y_done, NY * p + 2 * t + n + 1)
                                    cols = slice(n * FB, (n + 1) * FB)
                                    nc.vector.tensor_tensor(y[:, t, cols], y_bank[n][:, :],
                                                            y[:, t, cols], ALU.add
                                                            ).then_inc(y_added, 1)

                        def pair(p, more):
                            if isinstance(p, int) and p == 0:
                                hidden(p, 0, 0)
                            split2(p, 0)
                            split2(p, 1)
                            if not (isinstance(p, int) and p == 0):
                                hidden(p, 0, 0)
                            hidden(p, 0, 1)
                            if more:
                                split13(p + 1, 0)
                            hidden(p, 1, 0)
                            hidden(p, 1, 1)
                            for t in range(TT):
                                add_y(p, [t])
                                if more and t < T13:
                                    split13(p + 1, 1, [t])
                        split13(0, 0)
                        split13(0, 1)
                        pair(0, True)
                        with dve.Fori(1, NP - 1) as p:
                            pair(p, True)
                        pair(NP - 1, False)

                    @block.tensor
                    def _(pe):
                        def transpose13(p, par, n):
                            m, kh = n // 2, n % 2
                            pe.wait_ge(scaled13, 2 * (2 * p + par) + m + 1)
                            wait(pe, t_lo, t13_first(p, par) + n - 1)
                            for k in range(4):
                                kk = 4 * kh + k
                                last = pe.transpose(t_bank[n % 2][:, k * P:(k + 1) * P],
                                                    raw13[:, par, m, kk * P:(kk + 1) * P],
                                                    ident[:])
                            last.then_inc(t13_done, 1)

                        def transpose2(p, par, n):
                            pe.wait_ge(scaled2, 2 * p + par + 1)
                            wait(pe, t_lo, t2_first(p, par) + n - 1)
                            for k in range(4):
                                last = pe.transpose(t_bank[n % 2][:, k * P:(k + 1) * P],
                                                    raw2[:, par, 4 * n + k, :], ident[:])
                            last.then_inc(t2_done, 1)

                        def gate_up(p, par, tb, more):
                            n = 4 * p + 2 * par + tb
                            wait(pe, h_done, n - 1)
                            cols = slice(tb * TB, (tb + 1) * TB)
                            for m, (acc, done) in enumerate(((g_bank, g_done), (u_bank, u_done))):
                                for k in range(KT):
                                    if tb == 0 and k % 4 == 0:
                                        pe.wait_ge(t_lo, t13_first(p, par) + 2 * m + k // 4 + 1)
                                    last = split_product(
                                        pe, acc[tb][:, 0:TB],
                                        (w13_h[:, par, m, k, :], w13_l[:, par, m, k, :]),
                                        (x2_h[:, k, cols], x2_l[:, k, cols]), k == 0, k == KT - 1)
                                    if k % 4 == 1 and half == 0:
                                        n, start = 2 * m + k // 4, isinstance(p, int) and p == 0
                                        if par == 0 and tb == 0 and start:
                                            transpose13(0, 1, n)
                                        elif par == 0 and tb == (1 if start else 0):
                                            transpose2(p, n // T2, n % T2)
                                        elif par == 1 and tb == 0 and more:
                                            transpose13(p + 1, 0, n)
                                last.then_inc(done, 1)

                        def down(p, t):
                            pe.wait_ge(h_lo, 4 * p + (3 if (t + 1) * P <= TB else 4))
                            for n in range(2):
                                wait(pe, y_added, NY * p + 2 * t + n - 1)
                                rows, cols = slice(t * P, (t + 1) * P), slice(n * FB, (n + 1) * FB)
                                for par in range(2):
                                    last = split_product(
                                        pe, y_bank[n][:, :],
                                        (h_h[:, par, rows], h_l[:, par, rows]),
                                        (w2_h[:, par, cols], w2_l[:, par, cols]),
                                        par == 0, par == 1)
                                last.then_inc(y_done, 1)

                        def pair(p, more):
                            for par in range(2):
                                for tb in range(2):
                                    gate_up(p, par, tb, more)
                            pe.wait_ge(t_lo, t2_first(p, 1) + T2)
                            for t in range(TT):
                                down(p, t)
                                if more and t < T13 and half == 0:
                                    transpose13(p + 1, 1, t)
                        if half == 0:
                            for n in range(T13):
                                transpose13(0, 0, n)
                        pair(0, True)
                        with pe.Fori(1, NP - 1) as p:
                            pair(p, True)
                        pair(NP - 1, False)

        queries()
        attention()
        y = top.enter_context(nc.sbuf_tensor("y", [P, TT, D], f32))
        x2_h = top.enter_context(nc.sbuf_tensor("x2_h", [P, KT, HALF], f32r))
        x2_l = top.enter_context(nc.sbuf_tensor("x2_l", [P, KT, HALF], f32r))
        for half in range(2):
            mixing(half, y, x2_h, x2_l)
            ffn(half, y, x2_h, x2_l)


_INS = ['x', 'ctx_4096', 'L0_xattn_Wq', 'L0_xattn_Wk', 'L0_xattn_Wv', 'L0_xattn_Wo', 'L0_ffn_w1',
        'L0_ffn_w1_scale', 'L0_ffn_w3', 'L0_ffn_w3_scale', 'L0_ffn_w2', 'L0_ffn_w2_scale']


def kernel(**inputs):
    import numpy as _np
    import concourse.bacc as _bacc
    from concourse import mybir as _mybir
    from concourse.bass_utils import run_bass_kernel_spmd as _run

    nc = _bacc.Bacc("TRN2", target_bir_lowering=False, num_devices=1,
                     dynamic_dma_scratch_size=1024)
    arrays, args = {}, []
    for name in _INS:
        a = _np.ascontiguousarray(inputs[name])
        arrays[f"in_{name}"] = a
        args.append(nc.dram_tensor(f"in_{name}", a.shape, _mybir.dt.from_np(a.dtype),
                                   kind="ExternalInput").ap())
    out = nc.dram_tensor("out", arrays["in_x"].shape, _mybir.dt.float32, kind="ExternalOutput").ap()
    build_program(nc, *args, out)
    r = _run(nc, [arrays], core_ids=[0])
    return r.results[0]["out"]
```
